# Optimizing a Trainium2 kernel written in Bass

```python
import numpy as np
import jax
import jax.numpy as jnp

def _softmax(x, axis=-1):
    return jax.nn.softmax(x, axis=axis)
def _gelu(x):
    return jax.nn.gelu(x, approximate=True)
def _silu(x):
    return jax.nn.silu(x)
def _sigmoid(x):
    return jax.nn.sigmoid(x)
def _layernorm(x, axis=-1, eps=1e-5):
    m = jnp.mean(x, axis=axis, keepdims=True)
    v = jnp.var(x, axis=axis, keepdims=True)
    return (x - m) / jnp.sqrt(v + eps)
def _scatter_add(tgt, idx, src, axis=0):
    return tgt.at[idx].add(src)
def _segment_sum(src, seg, n):
    return jax.ops.segment_sum(src, seg, n)

kernel_name = 'mk_conv_preact_d2_conv_nhwc128_1a0757'

def setup_inputs(seed: int = 0):
    np.random.seed(seed)
    _w = jnp.asarray
    def _rec_inputs():
        import jax
        import jax.numpy as jnp
        _gk = jax.random.key(seed)
        x = -0.000125 + 0.9999 * jax.random.normal(jax.random.fold_in(_gk, 1), (16, 128, 128, 128), jnp.float32)
        return x
    x = _rec_inputs()
    def _L0_conv_setup():
        import jax, jax.numpy as jnp
        import numpy as np
        HEADS = 4
        DIM_HEAD = 32
        LN_EPS = 1e-05

        def _linear_attention(x, w_qkv, w_out, b_out, g_ln, b_ln):
            b, H, W, c = x.shape
            n = H * W
            scale = DIM_HEAD ** (-0.5)
            qkv = jnp.einsum('bxyc,cf->bxyf', x, w_qkv)
            q, k, v = jnp.split(qkv, 3, axis=-1)

            def to_bhdn(t):
                t = t.reshape(b, n, HEADS, DIM_HEAD)
                return jnp.transpose(t, (0, 2, 3, 1))
            q, k, v = (to_bhdn(q), to_bhdn(k), to_bhdn(v))
            q = jax.nn.softmax(q, axis=-2) * scale
            k = jax.nn.softmax(k, axis=-1)
            context = jnp.einsum('bhdn,bhen->bhde', k, v)
            out = jnp.einsum('bhde,bhdn->bhen', context, q)
            out = jnp.transpose(out, (0, 3, 1, 2)).reshape(b, H, W, HEADS * DIM_HEAD)
            out = jnp.einsum('bxyf,fc->bxyc', out, w_out) + b_out
            mean = jnp.mean(out, axis=-1, keepdims=True)
            var = jnp.mean(jnp.square(out - mean), axis=-1, keepdims=True)
            return (out - mean) / jnp.sqrt(var + LN_EPS) * g_ln + b_ln
        key = jax.random.key(seed)
        ks = jax.random.split(key, 3)
        b, H, W, c = (16, 128, 128, 128)
        hidden = HEADS * DIM_HEAD
        x = jax.random.normal(ks[0], (b, H, W, c), dtype=jnp.float32)
        w_qkv = jax.random.normal(ks[1], (c, 3 * hidden), dtype=jnp.float32) * (1.0 / np.sqrt(c))
        w_out = jax.random.normal(ks[2], (hidden, c), dtype=jnp.float32) * (1.0 / np.sqrt(hidden))
        b_out = jnp.zeros((c,), dtype=jnp.float32)
        g_ln = jnp.ones((1, 1, 1, c), dtype=jnp.float32)
        b_ln = jnp.zeros((1, 1, 1, c), dtype=jnp.float32)
        return {'x': x, 'w_qkv': w_qkv, 'w_out': w_out, 'b_out': b_out, 'g_ln': g_ln, 'b_ln': b_ln}
    _L0_conv_all = _L0_conv_setup()
    _L0_conv_in = {k: v for k, v in _L0_conv_all.items() if k in ('w_qkv', 'w_out', 'b_out', 'g_ln', 'b_ln', )}
    del _L0_conv_all

    def _L1_conv_setup():
        import jax, jax.numpy as jnp
        import numpy as np
        EPS = 1e-06

        def kernel_to_freq_2d(kernel, H, W):
            C, kh, kw = kernel.shape
            th = (jnp.arange(kh) - kh // 2) % H
            tw = (jnp.arange(kw) - kw // 2) % W
            TH, TW = jnp.meshgrid(th, tw, indexing='ij')
            padded = jnp.zeros((C, H, W), dtype=kernel.dtype).at[:, TH, TW].set(kernel)
            return jnp.fft.fft2(padded, axes=(1, 2))

        def heinsen_scan_log(log_coeffs, log_values):

            def op(left, right):
                la, lb = left
                ra, rb = right
                return (la + ra, jnp.logaddexp(ra + lb, rb))
            _, log_h = jax.lax.associative_scan(op, (log_coeffs, log_values), axis=0)
            return log_h
        key = jax.random.key(seed)
        ks = jax.random.split(key, 7)
        B, H, W, C, k = (4, 128, 128, 128, 7)
        fan_in = k * k
        x = jax.random.normal(ks[0], (B, H, W, C), dtype=jnp.float32)
        A_kernel = jax.random.normal(ks[1], (C, k, k), dtype=jnp.float32) / np.sqrt(fan_in)
        B_kernel = jax.random.normal(ks[2], (C, k, k), dtype=jnp.float32) / np.sqrt(fan_in)
        gate_A_kernel = jax.random.normal(ks[3], (C, k, k), dtype=jnp.float32) * 0.02
        gate_B_kernel = jax.random.normal(ks[4], (C, k, k), dtype=jnp.float32) * 0.02
        W_out = jax.random.normal(ks[5], (C, C), dtype=jnp.float32) / np.sqrt(C)
        b_out = jnp.zeros((C,), dtype=jnp.float32)
        return dict(x=x, A_kernel=A_kernel, B_kernel=B_kernel, gate_A_kernel=gate_A_kernel, gate_B_kernel=gate_B_kernel, W_out=W_out, b_out=b_out, T=8)
    _L1_conv_all = _L1_conv_setup()
    _L1_conv_in = {k: v for k, v in _L1_conv_all.items() if k in ('A_kernel', 'B_kernel', 'gate_A_kernel', 'gate_B_kernel', 'W_out', 'b_out', )}
    del _L1_conv_all

    return {
        "x": x,
        "L0_conv_w_qkv": _L0_conv_in["w_qkv"],
        "L0_conv_w_out": _L0_conv_in["w_out"],
        "L0_conv_b_out": _L0_conv_in["b_out"],
        "L0_conv_g_ln": _L0_conv_in["g_ln"],
        "L0_conv_b_ln": _L0_conv_in["b_ln"],
        "L1_conv_A_kernel": _L1_conv_in["A_kernel"],
        "L1_conv_B_kernel": _L1_conv_in["B_kernel"],
        "L1_conv_gate_A_kernel": _L1_conv_in["gate_A_kernel"],
        "L1_conv_gate_B_kernel": _L1_conv_in["gate_B_kernel"],
        "L1_conv_W_out": _L1_conv_in["W_out"],
        "L1_conv_b_out": _L1_conv_in["b_out"],
    }

def reference(x, L0_conv_w_qkv, L0_conv_w_out, L0_conv_b_out, L0_conv_g_ln, L0_conv_b_ln, L1_conv_A_kernel, L1_conv_B_kernel, L1_conv_gate_A_kernel, L1_conv_gate_B_kernel, L1_conv_W_out, L1_conv_b_out):
    import jax
    import jax.numpy as jnp
    def _L0_conv_ref(x, w_qkv, w_out, b_out, g_ln, b_ln):
        import jax, jax.numpy as jnp
        import numpy as np
        HEADS = 4
        DIM_HEAD = 32
        LN_EPS = 1e-05

        def _linear_attention(x, w_qkv, w_out, b_out, g_ln, b_ln):
            b, H, W, c = x.shape
            n = H * W
            scale = DIM_HEAD ** (-0.5)
            qkv = jnp.einsum('bxyc,cf->bxyf', x, w_qkv)
            q, k, v = jnp.split(qkv, 3, axis=-1)

            def to_bhdn(t):
                t = t.reshape(b, n, HEADS, DIM_HEAD)
                return jnp.transpose(t, (0, 2, 3, 1))
            q, k, v = (to_bhdn(q), to_bhdn(k), to_bhdn(v))
            q = jax.nn.softmax(q, axis=-2) * scale
            k = jax.nn.softmax(k, axis=-1)
            context = jnp.einsum('bhdn,bhen->bhde', k, v)
            out = jnp.einsum('bhde,bhdn->bhen', context, q)
            out = jnp.transpose(out, (0, 3, 1, 2)).reshape(b, H, W, HEADS * DIM_HEAD)
            out = jnp.einsum('bxyf,fc->bxyc', out, w_out) + b_out
            mean = jnp.mean(out, axis=-1, keepdims=True)
            var = jnp.mean(jnp.square(out - mean), axis=-1, keepdims=True)
            return (out - mean) / jnp.sqrt(var + LN_EPS) * g_ln + b_ln
        return _linear_attention(x, w_qkv, w_out, b_out, g_ln, b_ln)

    def _L1_conv_ref(x, A_kernel, B_kernel, gate_A_kernel, gate_B_kernel, W_out, b_out, T):
        import jax, jax.numpy as jnp
        import numpy as np
        EPS = 1e-06

        def kernel_to_freq_2d(kernel, H, W):
            C, kh, kw = kernel.shape
            th = (jnp.arange(kh) - kh // 2) % H
            tw = (jnp.arange(kw) - kw // 2) % W
            TH, TW = jnp.meshgrid(th, tw, indexing='ij')
            padded = jnp.zeros((C, H, W), dtype=kernel.dtype).at[:, TH, TW].set(kernel)
            return jnp.fft.fft2(padded, axes=(1, 2))

        def heinsen_scan_log(log_coeffs, log_values):

            def op(left, right):
                la, lb = left
                ra, rb = right
                return (la + ra, jnp.logaddexp(ra + lb, rb))
            _, log_h = jax.lax.associative_scan(op, (log_coeffs, log_values), axis=0)
            return log_h
        B, H, W, C = x.shape

        def ifft_real(z_bhwc):
            return jnp.fft.ifft2(z_bhwc.transpose(0, 3, 1, 2), axes=(2, 3)).real.transpose(0, 2, 3, 1)
        A_f = kernel_to_freq_2d(A_kernel, H, W).transpose(1, 2, 0)
        B_f = kernel_to_freq_2d(B_kernel, H, W).transpose(1, 2, 0)
        gA_f = kernel_to_freq_2d(gate_A_kernel, H, W).transpose(1, 2, 0)
        gB_f = kernel_to_freq_2d(gate_B_kernel, H, W).transpose(1, 2, 0)
        x_f = jnp.fft.fft2(x.transpose(0, 3, 1, 2), axes=(2, 3)).transpose(0, 2, 3, 1)
        gate_A = jax.nn.sigmoid(ifft_real(gA_f[None] * x_f))
        gate_B = jax.nn.sigmoid(ifft_real(gB_f[None] * x_f))
        a_spatial = ifft_real(jnp.broadcast_to(A_f[None], (B, H, W, C)))
        b_spatial = ifft_real(B_f[None] * x_f)
        a_t = a_spatial * gate_A
        b_t = b_spatial * gate_B
        gate_seq = jnp.tile(a_t[None], (T, 1, 1, 1, 1))
        h_tilde_seq = jnp.tile(b_t[None], (T, 1, 1, 1, 1))
        log_z = -jax.nn.softplus(-gate_seq)
        log_coeffs = -jax.nn.softplus(gate_seq)
        log_values = log_z + jnp.log(jax.nn.softplus(h_tilde_seq) + EPS)
        log_h = heinsen_scan_log(log_coeffs, log_values)
        h_final = jnp.exp(log_h[-1])
        return h_final @ W_out + b_out

    def _gn(v, G=32, eps=1e-5):
        B_, H_, W_, C_ = v.shape
        g = v.reshape(B_, H_, W_, G, C_ // G)
        m = jnp.mean(g, axis=(1, 2, 4), keepdims=True)
        s = jnp.var(g, axis=(1, 2, 4), keepdims=True)
        return ((g - m) / jnp.sqrt(s + eps)).reshape(v.shape)

    def _ln_c(v, eps=1e-6):
        m = jnp.mean(v, axis=-1, keepdims=True)
        s = jnp.var(v, axis=-1, keepdims=True)
        return (v - m) / jnp.sqrt(s + eps)

    def _ln_t(v, eps=1e-5):
        m = jnp.mean(v, axis=-1, keepdims=True)
        s = jnp.var(v, axis=-1, keepdims=True)
        return (v - m) / jnp.sqrt(s + eps)

    def _to_tokens(v):
        B_, H_, W_, C_ = v.shape
        return v.reshape(B_, H_ * W_, C_)
    def _from_tokens(t, like):
        return t.reshape(like.shape)

    x = x + _L0_conv_ref(_gn(x), L0_conv_w_qkv, L0_conv_w_out, L0_conv_b_out, L0_conv_g_ln, L0_conv_b_ln)
    x = x + _L1_conv_ref(_gn(x), L1_conv_A_kernel, L1_conv_B_kernel, L1_conv_gate_A_kernel, L1_conv_gate_B_kernel, L1_conv_W_out, L1_conv_b_out, 8)
    return x


_drawn_inputs = setup_inputs


def setup_inputs(seed=0):
    import zlib

    import numpy as np

    out = dict(_drawn_inputs(seed))
    spreads = {'L0_conv_b_out': (0.0, 0.1),
     'L0_conv_g_ln': (1.0, 0.2),
     'L0_conv_b_ln': (0.0, 0.1),
     'L1_conv_b_out': (0.0, 0.1)}
    factors = {'L1_conv_A_kernel': 8.0, 'L1_conv_gate_A_kernel': 8.0, 'L1_conv_gate_B_kernel': 4.47}
    for name, (base, spread) in spreads.items():
        noise = np.random.default_rng([zlib.crc32(name.encode()), seed]).standard_normal(out[name].shape)
        drawn = base * np.exp(spread * noise) if base else spread * noise
        out[name] = jnp.asarray(drawn.astype(out[name].dtype))
    for name, factor in factors.items():
        out[name] = (out[name] * factor).astype(out[name].dtype)
    return out
```

```python
from contextlib import ExitStack

import numpy as np

import concourse.bass as bass
from concourse import mybir

F32 = mybir.dt.float32
BF16 = mybir.dt.bfloat16
ALU = mybir.AluOpType
ACT = mybir.ActivationFunctionType
AX = mybir.AxisListType

P = 128
IMGS, HT, WD, C = 16, 128, 128, 128
N = HT * WD
HEADS, DH = 4, 32
GROUP = 4
GN_EPS, LN_EPS, H_EPS = 1e-5, 1e-5, 1e-6
KS = 7
TAPS = KS * KS
STEPS = 8
A_FREE = 1.0 - 0.5 ** STEPS

TPC = 8
CT = TPC * P
NCH = N // CT
ROWS_CH = CT // WD

STAT_T = 16
STAT_CH = N // (STAT_T * P)
STAT_RING = 4

BR, BC_ = 16, 8
NP_, NQ = HT // BR, WD // BC_
PADL = 3
WPAD = PADL + WD

QUADS = [(0, 0, 0, 0), (0, 1, 0, 2), (1, 0, 10, 0), (1, 1, 10, 2)]
QSIZE = [(BR - r0) * (BC_ - c0) for _, _, r0, c0 in QUADS]
QBASE = [0, 4 * QSIZE[0], 0, 4 * QSIZE[2]]
WIDE = 4 * (QSIZE[0] + QSIZE[1])
NARROW = 4 * (QSIZE[2] + QSIZE[3])
NARROW_K = 6 * BC_
CB = 4
NBLK = C // CB
GCH = 16
NGRP = C // GCH
BPG = GCH // CB
ZI, ZJ = 2 * BR + 5, 2 * BC_ + 5


def selection_table():
    z = np.zeros((KS, KS, ZI, ZJ), np.float32)
    for u in range(KS):
        for v in range(KS):
            z[u, v, 21 - u, 13 - v] = 1.0
    table = np.zeros((P, ZI * ZJ), np.float32)
    table[:TAPS] = z.reshape(TAPS, ZI * ZJ)
    return table


def build(nc, x, w_qkv, w_out0, b_out0, g_ln, b_ln, kB, kGB, kA, kGA, w_out1, b_out1,
          ident_d, group_d, head_d, sel_d, out):
    x1_d = nc.dram_tensor("x1_scratch", (IMGS, HT, WPAD, C), F32).ap()
    wide_d = nc.dram_tensor("toeplitz_wide", (NBLK, P, CB * WIDE), BF16).ap()
    narrow_d = nc.dram_tensor("toeplitz_narrow", (NBLK, NARROW_K, CB * NARROW), BF16).ap()
    norm_d = nc.dram_tensor("norm_rows", (IMGS, 2, C), F32).ap()

    with ExitStack() as whole:
        def keep(name, shape, dt=F32):
            return whole.enter_context(nc.sbuf_tensor(name, shape, dt))

        ident = keep("ident", [P, P])
        group = keep("group", [P, P])
        bln_col = keep("bln_col", [P, 1])
        scale1 = keep("scale1", [P, IMGS])
        shift1 = keep("shift1", [P, IMGS])
        scale2 = keep("scale2", [P, IMGS])
        shift2 = keep("shift2", [P, IMGS])
        sums2 = keep("sums2", [P, 2, IMGS])
        corner = keep("corner", [P, KS, KS, IMGS])

        setup(nc, x, kB, kGB, ident_d, group_d, sel_d, b_ln, wide_d, narrow_d,
              ident, group, bln_col, scale1, shift1)
        layer0(nc, x, w_qkv, w_out0, b_out0, g_ln, head_d, x1_d, ident, scale1, shift1, sums2)
        corner_block(nc, kA, kGA, x1_d, norm_d, ident, group, bln_col, sums2, scale2, shift2, corner)
        layer1(nc, w_out1, b_out1, b_ln, x1_d, wide_d, narrow_d, norm_d, ident, corner, out)


class Tally:

    def __init__(self, eng, sem):
        self.eng, self.sem, self.n = eng, sem, 0

    def then(self, ins):
        ins.then_inc(self.sem, 1)
        self.n += 1
        self.eng.wait_ge(self.sem, self.n)


def setup(nc, x, kB, kGB, ident_d, group_d, sel_d, b_ln, wide_d, narrow_d,
          ident, group, bln_col, scale1, shift1):
    NB = BR * 2 + 6 * 2
    BANKS = 4
    with ExitStack() as ctx:
        sb = lambda n, s, d=F32: ctx.enter_context(nc.sbuf_tensor(n, s, d))
        ps = lambda n, s, d=F32: ctx.enter_context(nc.psum_tensor(n, s, d))
        sem = lambda n: ctx.enter_context(nc.semaphore(n))
        xs = sb("stat_x", [P, STAT_RING, STAT_T * C])
        sq = sb("stat_sq", [P, 2, STAT_T * C])
        ones = sb("stat_ones", [P, 1])
        self32 = sb("sel_f32", [P, ZI * ZJ])
        sel = sb("sel", [P, 14, ZI, BC_], BF16)
        taps = sb("taps", [P, 2, C])
        tap_hl = sb("tap_hl", [P, 4, C], BF16)
        table = sb("table", [P, GCH, WIDE + NARROW], BF16)
        sums = sb("sums1", [P, 2, IMGS])
        stat = sb("stat1", [P, 2, IMGS])
        var = sb("var1", [P, IMGS])
        half = sb("minus_half1", [P, IMGS])
        psT = [ps(f"psT{k}", [P, 512]) for k in range(BANKS)]
        psS = [ps(f"psS{k}", [P, 512]) for k in range(2)]
        psG = ps("psG1", [P, 512])

        s_const = sem("a_const")
        s_dve = sem("a_dve")
        s_ready = sem("a_taps_ready")
        s_trow = sem("a_table_row")
        s_tfree = [sem(f"a_table_bank_free{k}") for k in range(BANKS)]
        s_tstored = sem("a_table_stored")
        s_x = [sem(f"a_x_loaded{k}") for k in range(STAT_RING)]
        s_xfree = [sem(f"a_x_free{k}") for k in range(STAT_RING)]
        s_sq = sem("a_sq_ready")
        s_sums = sem("a_sums_done")
        s_stat = sem("a_stat")
        s_pow = sem("a_pow")
        block = ctx.enter_context(nc.Block())
        NCONST = 6

        rows = []
        for q, (dp, dq, r0, c0) in enumerate(QUADS):
            for r in range(r0, BR):
                rows.append((q, dp, dq, r, c0, (r - r0) * (BC_ - c0)))
        assert len(rows) == NB

        def evac(eng_copy, j, k):
            q, dp, dq, r, c0, off = rows[j]
            ns = BC_ - c0
            base = QBASE[q] if q < 2 else WIDE + QBASE[q]
            src = psT[k][:, 0:ns * 4 * GCH].rearrange("p (s m c) -> p c m s", m=4, c=GCH)
            dst = table[:, :, base:base + 4 * QSIZE[q]].rearrange("p c (m o) -> p c m o", m=4)[:, :, :, off:off + ns]
            return eng_copy(dst, src)

        @block.sync
        def _(sp):
            sp.wait_ge(s_dve, 1)
            for dst, src in ((ident[:], ident_d), (group[:], group_d), (self32[:], sel_d),
                             (taps[0:TAPS, 0, :], kB), (taps[0:TAPS, 1, :], kGB), (bln_col[:], b_ln)):
                sp.dma_start(dst, src).then_inc(s_const, 16)
            with sp.Fori(0, IMGS) as img:
                for n in range(STAT_CH):
                    k = n % STAT_RING
                    sp.wait_ge(s_xfree[k], img * (STAT_CH // STAT_RING) + n // STAT_RING)
                    src = x[img].rearrange("(n p t) c -> n p (t c)", p=P, t=STAT_T)[n]
                    sp.dma_start(xs[:, k, :], src).then_inc(s_x[k], 16)

        @block.gpsimd
        def _(pool):
            with pool.Fori(0, NGRP) as g:
                for k in range(BANKS):
                    pool.wait_ge(s_tfree[k], (g + 1) * (NB // BANKS))
                for b in range(BPG):
                    pool.dma_start(wide_d[g * BPG + b].rearrange("p (c e) -> p c e", c=CB),
                                   table[:, b * CB:(b + 1) * CB, 0:WIDE]).then_inc(s_tstored, 16)
                    pool.dma_start(narrow_d[g * BPG + b].rearrange("p (c e) -> p c e", c=CB),
                                   table[0:NARROW_K, b * CB:(b + 1) * CB, WIDE:WIDE + NARROW]
                                   ).then_inc(s_tstored, 16)
            pool.wait_ge(s_tstored, NGRP * BPG * 32)
            nc.gpsimd.memset(half[:], -0.5).then_inc(s_pow, 1)
            pool.wait_ge(s_pow, 1)
            pool.wait_ge(s_stat, 2)
            nc.gpsimd.tensor_tensor(scale1[:], var[:], half[:], ALU.pow).then_inc(s_pow, 1)

        @block.tensor
        def _(pe):
            pe.wait_ge(s_ready, 1)
            with pe.Fori(0, NGRP) as g:
                for j, (q, dp, dq, r, c0, off) in enumerate(rows):
                    k = j % BANKS
                    pe.wait_ge(s_tfree[k], g * (NB // BANKS) + j // BANKS)
                    i0 = 21 - (r + 6 - BR * dp)
                    for s in range(c0, BC_):
                        j0 = 13 - (s + 6 - BC_ * dq)
                        mm = nc.tensor.matmul(
                            psT[k][:, (s - c0) * 4 * GCH:(s - c0 + 1) * 4 * GCH],
                            sel[:, j0, i0:i0 + BR, :].rearrange("t i j -> t (i j)"), tap_hl[:, :, bass.ds(g * GCH, GCH)],
                            start=True, stop=True)
                    mm.then_inc(s_trow, 1)
            with pe.Fori(0, IMGS) as img:
                for n in range(STAT_CH):
                    k = n % STAT_RING
                    pe.wait_ge(s_x[k], 16 * (img * (STAT_CH // STAT_RING) + n // STAT_RING + 1))
                    for t in range(STAT_T):
                        nc.tensor.matmul(psS[0][:, bass.ds(img, 1)], xs[:, k, t * C:(t + 1) * C], ones[:],
                                         start=(n == 0 and t == 0), stop=(n == STAT_CH - 1 and t == STAT_T - 1))
                    pe.wait_ge(s_sq, img * STAT_CH + n + 1)
                    for t in range(STAT_T):
                        mm = nc.tensor.matmul(psS[1][:, bass.ds(img, 1)], sq[:, n % 2, t * C:(t + 1) * C],
                                              ones[:], start=(n == 0 and t == 0),
                                              stop=(n == STAT_CH - 1 and t == STAT_T - 1))
                    mm.then_inc(s_xfree[k], 1)
            pe.wait_ge(s_sums, 1)
            nc.tensor.matmul(psG[:, 0:2 * IMGS], group[:], sums[:].rearrange("p a b -> p (a b)"),
                             start=True, stop=True).then_inc(s_sums, 1)

        @block.scalar
        def _(act):
            with act.Fori(0, NGRP) as g:
                for j in range(1, NB, 2):
                    act.wait_ge(s_trow, g * NB + j + 1)
                    if j == 1:
                        act.wait_ge(s_tstored, g * (BPG * 32))
                    evac(nc.scalar.copy, j, j % BANKS).then_inc(s_tfree[j % BANKS], 1)
            with act.Fori(0, IMGS) as img:
                for n in range(STAT_CH):
                    k = n % STAT_RING
                    act.wait_ge(s_x[k], 16 * (img * (STAT_CH // STAT_RING) + n // STAT_RING + 1))
                    act.wait_ge(s_xfree[(n - 2) % STAT_RING], img * (STAT_CH // STAT_RING) + (n - 2) // STAT_RING + 1)
                    nc.scalar.activation(sq[:, n % 2, :], xs[:, k, :], ACT.Square).then_inc(s_sq, 1)

        @block.vector
        def _(dve):
            t = Tally(dve, s_dve)
            t.then(nc.vector.memset(taps[:], 0.0))
            t.then(nc.vector.memset(ones[:], 1.0))
            dve.wait_ge(s_const, 16 * NCONST)
            for j0 in range(14):
                t.then(nc.vector.tensor_copy(sel[:, j0], self32[:].rearrange("t (a b) -> t a b", b=ZJ)[:, :, j0:j0 + BC_]))
            t.then(nc.vector.tensor_scalar(taps[:, 0, :], taps[:, 0, :], 0.5, None, ALU.mult))
            t.then(nc.vector.tensor_copy(tap_hl[:, 0:2, :], taps[:]))
            nc.vector.tensor_tensor(tap_hl[:, 2:4, :], taps[:], tap_hl[:, 0:2, :],
                                    ALU.subtract).then_inc(s_ready, 1)
            with dve.Fori(0, NGRP) as g:
                for j in range(0, NB, 2):
                    dve.wait_ge(s_trow, g * NB + j + 1)
                    if j == 0:
                        dve.wait_ge(s_tstored, g * (BPG * 32))
                    evac(nc.vector.tensor_copy, j, j % BANKS).then_inc(s_tfree[j % BANKS], 1)
            for k in range(STAT_RING):
                dve.wait_ge(s_xfree[k], IMGS * STAT_CH // STAT_RING)
            t.then(nc.vector.tensor_copy(sums[:, 0, :], psS[0][:, 0:IMGS]))
            nc.vector.tensor_copy(sums[:, 1, :], psS[1][:, 0:IMGS]).then_inc(s_sums, 1)
            dve.wait_ge(s_sums, 2)
            norm_scale(nc, dve, t, psG, stat, var, s_stat)
            dve.wait_ge(s_pow, 2)
            t.then(nc.vector.scalar_tensor_tensor(shift1[:], stat[:, 0, :], -1.0, scale1[:],
                                                  ALU.mult, ALU.mult))


def norm_scale(nc, dve, t, psG, stat, var, s_stat):
    t.then(nc.vector.tensor_copy(stat[:].rearrange("p a b -> p (a b)"), psG[:, 0:2 * IMGS]))
    t.then(nc.vector.tensor_tensor(var[:], stat[:, 0, :], stat[:, 0, :], ALU.mult))
    ins = nc.vector.tensor_tensor(var[:], stat[:, 1, :], var[:], ALU.subtract)
    ins.then_inc(s_stat, 1)
    dve.wait_ge(s_stat, 1)
    nc.vector.tensor_scalar(var[:], var[:], 0.0, GN_EPS, ALU.max, ALU.add).then_inc(s_stat, 1)
    dve.wait_ge(s_stat, 2)


def layer0(nc, x, w_qkv, w_out0, b_out0, g_ln, head_d, x1_d, ident, scale1, shift1, sums2):
    with ExitStack() as ctx:
        sb = lambda n, s, d=F32: ctx.enter_context(nc.sbuf_tensor(n, s, d))
        ps = lambda n, s, d=F32: ctx.enter_context(nc.psum_tensor(n, s, d))
        sem = lambda n: ctx.enter_context(nc.semaphore(n))
        X = [sb(f"X{n}", [P, TPC, C]) for n in range(NCH)]
        gT = [sb(f"gT{k}", [C, CT]) for k in range(2)]
        ekT = [sb(f"ekT{k}", [P, CT]) for k in range(2)]
        ek = [sb(f"ek{k}", [P, TPC, P]) for k in range(2)]
        q = [sb(f"q{k}", [P, TPC, P]) for k in range(3)]
        qT = sb("qT", [P, CT])
        sqo = sb("sqo", [P, TPC, C])
        y = [sb(f"y{k}", [P, TPC, C]) for k in range(2)]
        sqx = [sb(f"sqx{k}", [P, TPC, C]) for k in range(2)]
        wqkv = sb("wqkv", [C, 3 * C])
        head = sb("head", [P, P])
        wo = sb("wo", [P, 2, C])
        brow = sb("brow", [P, 2, C])
        grow = sb("grow", [P, C])
        mean_w = sb("mean_w", [P, 2])
        ones = sb("ones0", [P, 1])
        nmax = sb("nmax", [P, NCH + 1])
        nmax_c = sb("nmax_c", [P, NCH])
        corr = sb("corr", [P, NCH])
        ksum_c = sb("ksum_c", [P, NCH])
        ksum = sb("ksum", [P, NCH + 1])
        acc = sb("acc", [P, C])
        accn = sb("accn", [P, C])
        ctxg = sb("ctxg", [C, P])
        ctxT = sb("ctxT", [P, P])
        M = sb("M", [P, 2, C])
        rk = sb("rk", [P, 1])
        qmax = sb("qmax", [P, 3, TPC * HEADS])
        qsum = sb("qsum", [P, 3, TPC * HEADS])
        qinv = sb("qinv", [P, 3, TPC * HEADS])
        vsum = sb("vsum", [P, 2, TPC])
        rstd = sb("rstd", [P, 2, TPC])
        half = sb("minus_half0", [P, TPC])
        ceps = sb("ceps", [P, TPC])
        norm = sb("norm0", [P, 2])
        parts = sb("parts", [P, 2, NCH])
        psX = ps("psX", [P, CT])
        psK = ps("psK", [P, CT])
        psW = ps("psW", [P, 2 * CT])

        s_const = sem("b_const")
        s_chain = sem("b_chain")
        s_x = [sem(f"b_x_loaded{n}") for n in range(NCH)]
        s_store = [sem(f"b_stored{n}") for n in range(NCH)]
        psx_ready = sem("b_psx_ready")
        psx_drained = sem("b_psx_drained")
        psk_ready = sem("b_psk_ready")
        k_exped = sem("b_k_exped")
        q_subbed = sem("b_q_subbed")
        s_nmc = sem("b_nmc")
        s_nmax = sem("b_nmax")
        s_corr = sem("b_corr")
        et_ready = sem("b_et_ready")
        ek_ready = sem("b_ek_ready")
        ctx_done = sem("b_ctx_done")
        acc_done = sem("b_acc_done")
        s_m = sem("b_m_steps")
        s_qmax = sem("b_qmax")
        s_qexp = sem("b_qexp")
        s_qsum = sem("b_qsum")
        s_qinv = sem("b_qinv")
        s_qn = sem("b_qn")
        o_ready = sem("b_o_ready")
        s_sqo = sem("b_sqo")
        s_vsum = sem("b_vsum")
        s_rstd1 = sem("b_rstd_a")
        s_rstd = sem("b_rstd")
        s_y = sem("b_y")
        s_x1 = sem("b_x1")
        s_sqx = sem("b_sqx")
        st_ready = sem("b_st_ready")
        st_taken = sem("b_st_taken")
        s_centred = sem("b_centred")
        s_half = sem("b_half")
        s_norm = sem("b_norm")
        s_mready = sem("b_m_ready")
        block = ctx.enter_context(nc.Block())
        NCONST = 5

        B_SLOTS, C_SLOTS = NCH + 2, NCH + 7
        seqT, seqQ, seq = {}, {}, 0
        for n in range(NCH):
            seqT[("k", n)] = seq
            seq += 1
        for n in range(C_SLOTS):
            if 0 <= n - 3 < NCH:
                seqQ[n - 3] = seq
                seq += 1
            if n < NCH:
                seqT[("q", n)] = seq
                seq += 1
        SEQ = seq

        def x_chunk(img, n):
            return x[img].rearrange("(n p t) c -> n p t c", p=P, t=TPC)[n]

        @block.sync
        def _(sp):
            for dst, src in ((wqkv[:], w_qkv), (head[:], head_d), (wo[:, 0, :], w_out0),
                             (brow[:, 0, :], b_out0.partition_broadcast(P)),
                             (grow[:], g_ln.partition_broadcast(P))):
                sp.dma_start(dst, src).then_inc(s_const, 16)
            for n in range(NCH):
                sp.dma_start(X[n][:], x_chunk(0, n)).then_inc(s_x[n], 16)

            def reload(img, n):
                sp.wait_ge(s_store[n], 32 * (img + 1))
                sp.wait_ge(st_ready, img * NCH + n + 1)
                sp.dma_start(X[n][:], x_chunk(img + 1, n)).then_inc(s_x[n], 16)

            def image(img, last):
                for n in range(NCH):
                    sp.wait_ge(s_x1, img * NCH + n + 1)
                    rows = x1_d[img, ROWS_CH * n:ROWS_CH * (n + 1)]
                    xn = X[n][:].rearrange("p t c -> p (t c)")
                    sp.dma_start(rows[:, PADL:PADL + WD, :].rearrange("h (w t) c -> h w (t c)", t=TPC),
                                 xn).then_inc(s_store[n], 16)
                    sp.dma_start(rows[:, 0:PADL, :], X[n][15:P:16, TPC - PADL:TPC, :]).then_inc(s_store[n], 16)
                    if not last and n >= 4:
                        reload(img, n - 4)
                if not last:
                    for n in range(NCH - 4, NCH):
                        reload(img, n)

            with sp.Fori(0, IMGS - 1) as img:
                image(img, False)
            image(IMGS - 1, True)
            for n in range(NCH):
                sp.wait_ge(s_store[n], 32 * IMGS)

        @block.tensor
        def _(pe):
            pe.wait_ge(s_const, 16 * NCONST)
            pe.wait_ge(s_chain, 10)

            def fill_psx(img, tiles, seq):
                pe.wait_ge(psx_drained, img * SEQ + seq)
                for t in range(TPC):
                    mm = nc.tensor.transpose(psX[:, t * P:(t + 1) * P], tiles(t), ident[:])
                mm.then_inc(psx_ready, 1)

            def turn_x(img, n, phase):
                pe.wait_ge(s_x[n], 16 * img + 16)
                fill_psx(img, lambda t: X[n][:, t, :], seqT[(phase, n)])

            def keys(img, n):
                pe.wait_ge(psx_drained, img * SEQ + seqT[("k", n)] + 1)
                if n == 0:
                    pe.wait_ge(q_subbed, img * NCH)
                else:
                    pe.wait_ge(k_exped, img * NCH + n)
                for hf in range(2):
                    mm = nc.tensor.matmul(psK[:, hf * 512:(hf + 1) * 512], wqkv[:, C:2 * C],
                                          gT[n % 2][:, hf * 512:(hf + 1) * 512], start=True, stop=True)
                mm.then_inc(psk_ready, 1)

            def turn_ek(img, n):
                pe.wait_ge(k_exped, img * NCH + n + 1)
                if n == 0:
                    pe.wait_ge(s_y, img * NCH)
                pe.wait_ge(ek_ready, img * NCH + n)
                for t in range(TPC):
                    mm = nc.tensor.transpose(psW[:, t * P:(t + 1) * P], ekT[n % 2][:, t * P:(t + 1) * P], ident[:])
                mm.then_inc(et_ready, 1)

            def context(img, n):
                pe.wait_ge(ek_ready, img * NCH + n + 1)
                pe.wait_ge(acc_done, img * NCH + max(n - 1, 0))
                for t in range(TPC):
                    mm = nc.tensor.matmul(psW[:, CT + 512 * (n % 2):CT + 512 * (n % 2) + C], ek[n % 2][:, t, :],
                                          X[n][:, t, :], start=(t == 0), stop=(t == TPC - 1))
                mm.then_inc(ctx_done, 1)

            def queries(img, n):
                pe.wait_ge(psx_drained, img * SEQ + seqT[("q", n)] + 1)
                if n == 0:
                    pe.wait_ge(k_exped, img * NCH + NCH)
                else:
                    pe.wait_ge(q_subbed, img * NCH + n)
                for t in range(TPC):
                    mm = nc.tensor.matmul(psK[:, t * P:(t + 1) * P], gT[n % 2][:, t * P:(t + 1) * P],
                                          wqkv[:, 0:C], start=True, stop=True)
                mm.then_inc(psk_ready, 1)

            def turn_q(img, n):
                pe.wait_ge(s_qn, img * NCH + n + 1)
                fill_psx(img, lambda t: q[n % 3][:, t, :], seqQ[n])

            def project(img, n):
                pe.wait_ge(psx_drained, img * SEQ + seqQ[n] + 1)
                pe.wait_ge(s_y, img * NCH + n)
                for t in range(TPC):
                    mm = nc.tensor.matmul(psW[:, t * 2 * C:(t + 1) * 2 * C], qT[:, t * P:(t + 1) * P],
                                          M[:].rearrange("p a c -> p (a c)"), start=True, stop=True)
                mm.then_inc(o_ready, 1)

            def sums(img, n, seq_before):
                pe.wait_ge(psx_drained, img * SEQ + seq_before)
                pe.wait_ge(s_sqx, img * NCH + n + 1)
                pe.wait_ge(st_taken, img * NCH + n)
                for a, src in enumerate((X[n], sqx[n % 2])):
                    for t in range(TPC):
                        mm = nc.tensor.matmul(psX[:, 512 * a:512 * a + 1], src[:, t, :], ones[:],
                                              start=(t == 0), stop=(t == TPC - 1))
                mm.then_inc(st_ready, 1)

            with pe.Fori(0, IMGS) as img:
                for n in range(B_SLOTS):
                    if 0 <= n - 1 < NCH:
                        keys(img, n - 1)
                    if n < NCH:
                        if n == 0:
                            pe.wait_ge(st_taken, img * NCH)
                        turn_x(img, n, "k")
                    if 0 <= n - 2 < NCH:
                        context(img, n - 2)
                    if 0 <= n - 1 < NCH:
                        turn_ek(img, n - 1)
                pe.wait_ge(s_m, img * 7 + 2)
                nc.tensor.transpose(psW[:, 0:P], accn[:], ident[:]).then_inc(s_m, 1)
                pe.wait_ge(s_m, img * 7 + 4)
                nc.tensor.matmul(psW[:, 512:512 + P], wqkv[:, 2 * C:3 * C], ctxg[:], start=True, stop=True
                                 ).then_inc(s_m, 1)
                pe.wait_ge(s_m, img * 7 + 6)
                nc.tensor.matmul(psW[:, 1024:1024 + 2 * C], ctxT[:], wo[:].rearrange("p a c -> p (a c)"),
                                 start=True, stop=True).then_inc(s_m, 1)
                psx_used = NCH
                taken = 0
                for n in range(C_SLOTS):
                    if 0 <= n - 3 < NCH:
                        pe.wait_ge(st_taken, img * NCH + taken)
                        turn_q(img, n - 3)
                        psx_used += 1
                    if 0 <= n - 1 < NCH:
                        queries(img, n - 1)
                    if n < NCH:
                        if n - 3 < 0:
                            pe.wait_ge(st_taken, img * NCH + taken)
                        turn_x(img, n, "q")
                        psx_used += 1
                    if 0 <= n - 3 < NCH:
                        if n == 3:
                            pe.wait_ge(s_mready, img + 1)
                        project(img, n - 3)
                    if 0 <= n - 6 < NCH:
                        sums(img, n - 6, psx_used)
                        taken += 1

        @block.scalar
        def _(act):
            def norm_out(img, n, phase, g):
                act.wait_ge(psx_ready, img * SEQ + seqT[(phase, n)] + 1)
                act.wait_ge(psk_ready, img * 2 * NCH + max(g - 1, 0))
                nc.scalar.activation(gT[n % 2][:], psX[:], ACT.Identity, bias=norm[:, 1:2],
                                     scale=norm[:, 0:1]).then_inc(psx_drained, 1)

            def exp_k(img, n):
                act.wait_ge(s_nmax, img * NCH + n + 1)
                act.wait_ge(et_ready, img * NCH + max(n - 1, 0))
                nc.scalar.activation(ekT[n % 2][:], psK[:], ACT.Exp, bias=nmax[:, n + 1:n + 2],
                                     accum_out=ksum_c[:, n:n + 1]).then_inc(k_exped, 1)
                nc.scalar.activation(corr[:, n:n + 1], nmax[:, n:n + 1], ACT.Exp, bias=nmax[:, n + 1:n + 2],
                                     scale=-1.0).then_inc(s_corr, 1)

            with act.Fori(0, IMGS) as img:
                act.wait_ge(s_norm, img + 1)
                for n in range(B_SLOTS):
                    if n < NCH:
                        norm_out(img, n, "k", n)
                    if 0 <= n - 1 < NCH:
                        exp_k(img, n - 1)
                act.wait_ge(s_m, img * 7 + 3)
                nc.scalar.activation(ctxg[:], psW[:, 0:P], ACT.Identity, bias=norm[:, 1:2],
                                     scale=norm[:, 0:1]).then_inc(s_m, 1)
                for n in range(C_SLOTS):
                    if 0 <= n - 4 < NCH:
                        act.wait_ge(o_ready, img * NCH + n - 4 + 1)
                        act.wait_ge(s_vsum, img * NCH + n - 4)
                        nc.scalar.activation(sqo[:], psW[:].rearrange("p (t a c) -> p t a c", t=TPC, a=2)[:, :, 0, :],
                                             ACT.Square).then_inc(s_sqo, 1)
                    if 0 <= n - 3 < NCH:
                        act.wait_ge(psx_ready, img * SEQ + seqQ[n - 3] + 1)
                        act.wait_ge(o_ready, img * NCH + n - 3)
                        nc.scalar.copy(qT[:], psX[:]).then_inc(psx_drained, 1)
                    if n < NCH:
                        norm_out(img, n, "q", NCH + n)
                    if 0 <= n - 1 < NCH:
                        act.wait_ge(q_subbed, img * NCH + n - 1 + 1)
                        nc.scalar.activation(q[(n - 1) % 3][:], q[(n - 1) % 3][:], ACT.Exp).then_inc(s_qexp, 1)
                    if 0 <= n - 5 < NCH:
                        act.wait_ge(s_x1, img * NCH + n - 5 + 1)
                        act.wait_ge(st_ready, img * NCH + max(n - 5 - 1, 0))
                        nc.scalar.activation(sqx[(n - 5) % 2][:], X[n - 5][:], ACT.Square).then_inc(s_sqx, 1)

        @block.vector
        def _(dve):
            t = Tally(dve, s_chain)
            t.then(nc.vector.memset(ones[:], 1.0))
            t.then(nc.vector.memset(acc[:], 0.0))
            t.then(nc.vector.memset(nmax[:, 0:1], 3.0e38))
            t.then(nc.vector.memset(ksum[:, 0:1], 0.0))
            dve.wait_ge(s_const, 16 * NCONST)
            t.then(nc.vector.tensor_reduce(mean_w[:, 0:1], wo[:, 0, :], AX.X, ALU.add))
            t.then(nc.vector.tensor_reduce(mean_w[:, 1:2], brow[:, 0, :], AX.X, ALU.add))
            t.then(nc.vector.tensor_scalar(mean_w[:], mean_w[:], 1.0 / C, None, ALU.mult))
            for src, i, f in ((wo, 0, 1.0), (brow, 1, 1.0 / HEADS)):
                ins = nc.vector.tensor_scalar(src[:, 0, :], src[:, 0, :], mean_w[:, i:i + 1], f,
                                              ALU.subtract, ALU.mult)
                ins.then_inc(s_centred, 1)
            dve.wait_ge(s_centred, 2)
            t.then(nc.vector.tensor_scalar(grow[:], grow[:], float(np.sqrt(C)), None, ALU.mult))
            t.then(nc.vector.tensor_tensor(wo[:, 1, :], wo[:, 0, :], grow[:], ALU.mult))
            t.then(nc.vector.tensor_tensor(brow[:, 1, :], brow[:, 0, :], grow[:], ALU.mult))

            def max_k(img, n):
                dve.wait_ge(psk_ready, img * 2 * NCH + n + 1)
                nc.vector.tensor_reduce(nmax_c[:, n:n + 1], psK[:], AX.X, ALU.max, negate=True).then_inc(s_nmc, 1)
                dve.wait_ge(s_nmc, img * NCH + n + 1)
                dve.wait_ge(s_nmax, img * NCH + n)
                nc.vector.tensor_tensor(nmax[:, n + 1:n + 2], nmax[:, n:n + 1], nmax_c[:, n:n + 1],
                                        ALU.min).then_inc(s_nmax, 1)

            def copy_ek(img, n):
                dve.wait_ge(et_ready, img * NCH + n + 1)
                dve.wait_ge(ctx_done, img * NCH + max(n - 1, 0))
                nc.vector.tensor_copy(ek[n % 2][:].rearrange("p t c -> p (t c)"), psW[:, 0:CT]).then_inc(ek_ready, 1)

            def add_up(img, n):
                dve.wait_ge(ctx_done, img * NCH + n + 1)
                dve.wait_ge(s_corr, img * NCH + n + 1)
                dve.wait_ge(acc_done, img * NCH + n)
                nc.vector.scalar_tensor_tensor(ksum[:, n + 1:n + 2], ksum[:, n:n + 1], corr[:, n:n + 1],
                                               ksum_c[:, n:n + 1], ALU.mult, ALU.add)
                nc.vector.scalar_tensor_tensor(
                    acc[:], acc[:], corr[:, n:n + 1], psW[:, CT + 512 * (n % 2):CT + 512 * (n % 2) + C],
                    ALU.mult, ALU.add).then_inc(acc_done, 1)

            with dve.Fori(0, IMGS) as img:
                nc.vector.tensor_copy(norm[:, 0:1], scale1[:, bass.ds(img, 1)])
                nc.vector.tensor_copy(norm[:, 1:2], shift1[:, bass.ds(img, 1)]).then_inc(s_norm, 1)
                for n in range(B_SLOTS):
                    if 0 <= n - 1 < NCH:
                        max_k(img, n - 1)
                    if 0 <= n - 2 < NCH:
                        add_up(img, n - 2)
                    if 0 <= n - 1 < NCH:
                        copy_ek(img, n - 1)
                dve.wait_ge(acc_done, img * NCH + NCH)
                nc.vector.reciprocal(rk[:], ksum[:, NCH:NCH + 1]).then_inc(s_m, 1)
                dve.wait_ge(s_m, img * 7 + 1)
                nc.vector.tensor_scalar(accn[:], acc[:], rk[:], None, ALU.mult).then_inc(s_m, 1)
                dve.wait_ge(s_m, img * 7 + 5)
                nc.vector.tensor_tensor(ctxT[:], psW[:, 512:512 + P], head[:], ALU.mult).then_inc(s_m, 1)
                dve.wait_ge(s_m, img * 7 + 7)
                nc.vector.tensor_tensor(M[:].rearrange("p a c -> p (a c)"), psW[:, 1024:1024 + 2 * C],
                                        brow[:].rearrange("p a c -> p (a c)"), ALU.add).then_inc(s_mready, 1)
                for n in range(C_SLOTS + 1):
                    if 0 <= n - 7 < NCH:
                        m = n - 7
                        dve.wait_ge(st_ready, img * NCH + m + 1)
                        nc.vector.tensor_copy(parts[:, :, m], psX[:, 0:CT:512]).then_inc(st_taken, 1)
                    if 0 <= n - 4 < NCH:
                        m = n - 4
                        dve.wait_ge(s_sqo, img * NCH + m + 1)
                        nc.vector.tensor_reduce(vsum[:, m % 2, :], sqo[:], AX.X, ALU.add).then_inc(s_vsum, 1)
                    if 0 <= n - 1 < NCH:
                        m = n - 1
                        dve.wait_ge(psk_ready, img * 2 * NCH + NCH + m + 1)
                        v = psK[:].rearrange("p (h d) -> p h d", d=DH)
                        nc.vector.tensor_reduce(qmax[:, m % 3, :], v, AX.X, ALU.max).then_inc(s_qmax, 1)
                        dve.wait_ge(s_qmax, img * NCH + m + 1)
                        dve.wait_ge(psx_ready, img * SEQ + (seqQ[m - 3] + 1 if m >= 3 else 0))
                        qv = q[m % 3][:].rearrange("p t (h d) -> p (t h) d", d=DH)
                        mx = qmax[:, m % 3, :].unsqueeze(2).to_broadcast([P, TPC * HEADS, DH])
                        nc.vector.tensor_tensor(qv, v, mx, ALU.subtract).then_inc(q_subbed, 1)
                    if 0 <= n - 4 < NCH:
                        m = n - 4
                        dve.wait_ge(s_rstd, img * NCH + m + 1)
                        dve.wait_ge(s_x1, img * NCH + max(m - 1, 0))
                        rs = rstd[:, m % 2, :].unsqueeze(2).to_broadcast([P, TPC, C])
                        nc.vector.tensor_tensor(y[m % 2][:], psW[:].rearrange("p (t a c) -> p t a c", t=TPC, a=2)[:, :, 1, :],
                                                rs, ALU.mult).then_inc(s_y, 1)
                    if 0 <= n - 1 < NCH:
                        m = n - 1
                        dve.wait_ge(s_qexp, img * NCH + m + 1)
                        qv = q[m % 3][:].rearrange("p t (h d) -> p (t h) d", d=DH)
                        nc.vector.tensor_reduce(qsum[:, m % 3, :], qv, AX.X, ALU.add).then_inc(s_qsum, 1)
                        dve.wait_ge(s_qsum, img * NCH + m + 1)
                        nc.vector.reciprocal(qinv[:, m % 3, :], qsum[:, m % 3, :]).then_inc(s_qinv, 1)
                dve.wait_ge(st_taken, img * NCH + NCH)
                nc.vector.tensor_reduce(sums2[:, :, bass.ds(img, 1)], parts[:], AX.X, ALU.add)

        @block.gpsimd
        def _(pool):
            nc.gpsimd.memset(half[:], -0.5).then_inc(s_half, 1)
            nc.gpsimd.memset(ceps[:], C * LN_EPS).then_inc(s_half, 1)
            pool.wait_ge(s_half, 2)
            with pool.Fori(0, IMGS) as img:
                for n in range(C_SLOTS):
                    if 0 <= n - 4 < NCH:
                        m = n - 4
                        pool.wait_ge(s_vsum, img * NCH + m + 1)
                        nc.gpsimd.tensor_tensor(rstd[:, m % 2, :], vsum[:, m % 2, :], ceps[:],
                                                ALU.add).then_inc(s_rstd1, 1)
                        pool.wait_ge(s_rstd1, img * NCH + m + 1)
                        nc.gpsimd.tensor_tensor(rstd[:, m % 2, :], rstd[:, m % 2, :], half[:],
                                                ALU.pow).then_inc(s_rstd, 1)
                    if 0 <= n - 2 < NCH:
                        m = n - 2
                        pool.wait_ge(s_qinv, img * NCH + m + 1)
                        qv = q[m % 3][:].rearrange("p t (h d) -> p (t h) d", d=DH)
                        iv = qinv[:, m % 3, :].unsqueeze(2).to_broadcast([P, TPC * HEADS, DH])
                        nc.gpsimd.tensor_tensor(qv, qv, iv, ALU.mult).then_inc(s_qn, 1)
                    if 0 <= n - 4 < NCH:
                        m = n - 4
                        pool.wait_ge(s_y, img * NCH + m + 1)
                        nc.gpsimd.tensor_tensor(X[m][:], X[m][:], y[m % 2][:], ALU.add).then_inc(s_x1, 1)


def corner_block(nc, kA, kGA, x1_d, norm_d, ident, group, bln_col, sums2, scale2, shift2, corner):
    HW_ = KS - 1
    WIN = 2 * HW_ + 1
    LO, HI = HW_ * WIN, (HW_ + 1) * WIN
    FLAT = KS * KS * IMGS
    with ExitStack() as ctx:
        sb = lambda n, s, d=F32: ctx.enter_context(nc.sbuf_tensor(n, s, d))
        ps = lambda n, s, d=F32: ctx.enter_context(nc.psum_tensor(n, s, d))
        sem = lambda n: ctx.enter_context(nc.semaphore(n))
        tok = sb("tok", [P, 2, 2, C])
        win = sb("win", [C, WIN, WIN, IMGS])
        gate = sb("gate", [C, KS, KS, IMGS])
        a = sb("a", [C, KS, KS, IMGS])
        cpow = sb("cpow", [C, KS, KS, IMGS])
        cp1 = sb("cp1", [C, KS, KS, IMGS])
        ka = sb("ka", [C, TAPS])
        kga = sb("kga", [C, TAPS])
        stat = sb("stat2", [P, 2, IMGS])
        var = sb("var2", [P, IMGS])
        cross = sb("cross", [P, IMGS])
        bb = sb("bb", [P, 2])
        half = sb("minus_half2", [P, IMGS])
        rows = sb("norm_rows_sb", [IMGS, 2, C])
        psG = ps("psG2", [P, 512])
        psR = ps("psR", [P, 2, 128])
        psT = [ps(f"psTok{k}", [P, 2, P]) for k in range(2)]
        s_const = sem("c_const")
        s_chain = sem("c_chain")
        s_sums = sem("c_sums")
        s_stat = sem("c_stat")
        s_pow = sem("c_pow")
        s_norm = sem("c_norm_ready")
        s_rows = sem("c_rows")
        s_rout = sem("c_rows_out")
        s_tok = [sem(f"c_tok{k}") for k in range(2)]
        s_turned = sem("c_turned")
        s_win = [sem(f"c_win{k}") for k in range(2)]
        s_gate = sem("c_gate")
        s_sig = sem("c_sigmoids")
        block = ctx.enter_context(nc.Block())

        @block.sync
        def _(sp):
            sp.dma_start(ka[:], kA).then_inc(s_const, 16)
            sp.dma_start(kga[:], kGA).then_inc(s_const, 16)
            for pair in range(IMGS // 2):
                for k in range(2):
                    sp.wait_ge(s_win[k], pair * 4)
                    im = x1_d[pair * 2 + k]
                    left, right = slice(PADL + WD - HW_, PADL + WD), slice(PADL, PADL + HW_ + 1)
                    for dst, r, c in ((tok[0:HW_ * HW_, k, 0, :], slice(HT - HW_, HT), left),
                                      (tok[HW_ * HW_:LO, k, 0, :], slice(HT - HW_, HT), right),
                                      (tok[0:KS * HW_, k, 1, :], slice(0, KS), left),
                                      (tok[KS * HW_:HI, k, 1, :], slice(0, KS), right)):
                        sp.dma_start(dst, im[r, c, :]).then_inc(s_tok[k], 16)
            sp.wait_ge(s_rows, 2)
            sp.dma_start(norm_d, rows[:]).then_inc(s_rout, 16)
            sp.wait_ge(s_rout, 16)

        @block.gpsimd
        def _(pool):
            nc.gpsimd.memset(half[:], -0.5).then_inc(s_pow, 1)
            pool.wait_ge(s_pow, 1)
            pool.wait_ge(s_stat, 2)
            nc.gpsimd.tensor_tensor(scale2[:], var[:], half[:], ALU.pow).then_inc(s_pow, 1)

        @block.tensor
        def _(pe):
            pe.wait_ge(s_sums, 1)
            nc.tensor.matmul(psG[:, 0:2 * IMGS], group[:], stat[:].rearrange("p a b -> p (a b)"),
                             start=True, stop=True).then_inc(s_sums, 1)
            pe.wait_ge(s_norm, 1)
            nc.tensor.transpose(psR[0:IMGS, 0, :], scale2[:], ident[:])
            nc.tensor.transpose(psR[0:IMGS, 1, :], shift2[:], ident[:]).then_inc(s_rows, 1)
            for pair in range(IMGS // 2):
                for k in range(2):
                    pe.wait_ge(s_tok[k], pair * 64 + 64)
                    pe.wait_ge(s_win[k], pair * 4)
                    nc.tensor.transpose(psT[k][:, 0, 0:LO], tok[0:LO, k, 0, :], ident[0:LO, 0:LO])
                    nc.tensor.transpose(psT[k][:, 1, 0:HI], tok[0:HI, k, 1, :], ident[0:HI, 0:HI]
                                        ).then_inc(s_turned, 1)

        @block.scalar
        def _(act):
            act.wait_ge(s_norm, 1)
            for pair in range(IMGS // 2):
                for k in range(2):
                    img = pair * 2 + k
                    act.wait_ge(s_turned, pair * 2 + k + 1)
                    for half_, rows_, nr in ((0, slice(0, HW_), HW_), (1, slice(HW_, WIN), KS)):
                        for at, cols, ncol in ((0, slice(0, HW_), HW_), (nr * HW_, slice(HW_, WIN), KS)):
                            src = psT[k][:, half_, at:at + nr * ncol].rearrange("p (r c) -> p r c", c=ncol)
                            nc.scalar.activation(win[:, rows_, cols, img], src, ACT.Identity,
                                                 bias=shift2[:, img:img + 1], scale=scale2[:, img:img + 1]
                                                 ).then_inc(s_win[k], 1)
            flat = lambda z: z[:].rearrange("p a b i -> p (a b i)")
            act.wait_ge(s_gate, TAPS)
            nc.scalar.activation(flat(gate), flat(gate), ACT.Sigmoid).then_inc(s_sig, 1)
            act.wait_ge(s_gate, TAPS + 1)
            nc.scalar.activation(flat(cpow), flat(a), ACT.Sigmoid, scale=-1.0).then_inc(s_sig, 1)
            nc.scalar.activation(flat(corner), flat(a), ACT.Sigmoid).then_inc(s_sig, 1)

        @block.vector
        def _(dve):
            t = Tally(dve, s_chain)
            bln = lambda: bln_col[:]
            t.then(nc.vector.tensor_scalar(cross[:], sums2[:, 0, :], bln(), 2.0, ALU.mult, ALU.mult))
            t.then(nc.vector.tensor_tensor(cross[:], sums2[:, 1, :], cross[:], ALU.add))
            t.then(nc.vector.tensor_scalar(bb[:, 0:1], bln(), float(N), None, ALU.mult))
            t.then(nc.vector.tensor_tensor(bb[:, 1:2], bb[:, 0:1], bln(), ALU.mult))
            t.then(nc.vector.tensor_scalar(stat[:, 0, :], sums2[:, 0, :], bb[:, 0:1], None, ALU.add))
            nc.vector.tensor_scalar(stat[:, 1, :], cross[:], bb[:, 1:2], None, ALU.add).then_inc(s_sums, 1)
            dve.wait_ge(s_sums, 2)
            norm_scale(nc, dve, t, psG, stat, var, s_stat)
            dve.wait_ge(s_pow, 2)
            t.then(nc.vector.tensor_scalar(stat[:, 0, :], stat[:, 0, :], bln(), -1.0, ALU.subtract, ALU.mult))
            nc.vector.tensor_tensor(shift2[:], stat[:, 0, :], scale2[:], ALU.mult).then_inc(s_norm, 1)
            dve.wait_ge(s_rows, 1)
            nc.vector.tensor_copy(rows[:], psR[0:IMGS, :, :]).then_inc(s_rows, 1)
            dve.wait_ge(s_const, 32)
            for k in range(2):
                dve.wait_ge(s_win[k], 4 * (IMGS // 2))
            for u in range(KS):
                for v in range(KS):
                    i = u * KS + v
                    src = win[:, HW_ - u:HW_ - u + KS, HW_ - v:HW_ - v + KS, :].rearrange("p a b i -> p a (b i)")
                    dst = gate[:].rearrange("p a b i -> p a (b i)")
                    if i == 0:
                        ins = nc.vector.tensor_scalar(dst, src, kga[:, 0:1], None, ALU.mult)
                    else:
                        dve.wait_ge(s_gate, i)
                        ins = nc.vector.scalar_tensor_tensor(dst, src, kga[:, i:i + 1], dst, ALU.mult, ALU.add)
                    ins.then_inc(s_gate, 1)
            f3 = lambda z: z[:].rearrange("p a b i -> p (a b) i")
            dve.wait_ge(s_sig, 1)
            nc.vector.tensor_tensor(f3(a), f3(gate), ka[:].unsqueeze(2).to_broadcast([C, TAPS, IMGS]),
                                    ALU.mult).then_inc(s_gate, 1)
            dve.wait_ge(s_sig, 3)
            flat = lambda z: z[:].rearrange("p a b i -> p (a b i)")
            for i in range(3):
                t.then(nc.vector.tensor_scalar(flat(cp1), flat(cpow), 1.0, 1.0 if i else 1.0 / A_FREE,
                                               ALU.add, ALU.mult))
                t.then(nc.vector.tensor_tensor(flat(corner), flat(corner), flat(cp1), ALU.mult))
                t.then(nc.vector.tensor_tensor(flat(cpow), flat(cpow), flat(cpow), ALU.mult))


def layer1(nc, w_out1, b_out1, b_ln, x1_d, wide_d, narrow_d, norm_d, ident, corner, out):
    HQ = [(0, 8), (8, 8)]
    NST = 2 * (NP_ + 1)
    RES = 4
    with ExitStack() as ctx:
        sb = lambda n, s, d=F32: ctx.enter_context(nc.sbuf_tensor(n, s, d))
        ps = lambda n, s, d=F32: ctx.enter_context(nc.psum_tensor(n, s, d))
        sem = lambda n: ctx.enter_context(nc.semaphore(n))
        xhl = sb("xhl", [P, 2, NP_ + 1, NQ, C], BF16)
        right = sb("right", [P, 2, 2, (NP_ + 1) * NQ, CB], BF16)
        h = sb("h", [P, BR * BC_, C])
        wide = sb("wide", [P, 2, CB, WIDE], BF16)
        narrow = sb("narrow", [P, 2, CB, NARROW], BF16)
        stage = [sb(f"stage{k}", [P, HQ[k][1], C]) for k in range(2)]
        tbuf = sb("tbuf", [P, 2, GCH, P])
        ubuf = sb("ubuf", [P, GCH, P])
        nrow = sb("nrow", [P, 2, C])
        w = sb("w1", [C, C])
        bias = sb("bias", [1, C])
        bl = sb("bl", [1, C])
        bias3 = sb("bias3", [1, 3, C], BF16)
        ones3 = sb("ones3", [1, P], BF16)
        psC = [ps(f"psC{k}", [P, CB, 2, P]) for k in range(2)]
        psH = ps("psH", [C, BC_, P])
        psO = ps("psO", [P, BC_ * C])

        s_const = sem("d_const")
        s_chain = sem("d_chain")
        s_bias = sem("d_bias")
        s_t = [sem(f"d_table{k}") for k in range(2)]
        s_st = [sem(f"d_stage{k}") for k in range(2)]
        s_nrow = sem("d_nrow")
        s_right = sem("d_right")
        s_res = [sem(f"d_res{k}") for k in range(RES)]
        s_out = [sem(f"d_out{k}") for k in range(RES)]
        s_scaled = sem("d_scaled")
        s_normed = sem("d_normed")
        xh_done = sem("d_xh")
        xl_done = sem("d_xl")
        conv_ready = sem("d_conv")
        th_done = sem("d_tanh")
        s_prod = [sem(f"d_prod{k}") for k in range(2)]
        s_nabs = sem("d_nabs")
        s_exp = sem("d_exp")
        s_ln = sem("d_ln")
        h_done = sem("d_h")
        ht_ready = sem("d_ht_ready")
        ht_evac = sem("d_ht_evac")
        s_fixed = sem("d_fixed")
        o_ready = sem("d_o_ready")
        s_added = sem("d_added")
        block = ctx.enter_context(nc.Block())

        res = tbuf[:].rearrange("p a g c -> p (a g c)").rearrange("p (k e) -> p k e", k=RES)
        hT = ubuf[:].rearrange("p g c -> p (g c)").rearrange("p (k e) -> p k e", k=2)
        FIX = {HT - 3 + y - (NP_ - 1) * BR if y < 3 else y - 3: (NP_ - 1 if y < 3 else 0, y) for y in range(KS)}

        def stage_parts(img, pr, q0, nq):
            im = x1_d[img]
            cols = slice(q0 * BC_, (q0 + nq) * BC_)
            parts = []

            def by_row(i, hrow):
                parts.append((slice(i * BC_, (i + 1) * BC_), im[hrow, cols, :].rearrange("(q j) c -> j q c", j=BC_)))

            def by_col(i0, n, hrow):
                for j in range(BC_):
                    parts.append((slice(i0 * BC_ + j, (i0 + n - 1) * BC_ + j + 1, BC_),
                                  im[hrow:hrow + n, cols, :].rearrange("h (q j) c -> h j q c", j=BC_)[:, j]))
            if pr == 0:
                for i in range(PADL):
                    by_row(i, HT - PADL + i)
                by_col(PADL, BR - PADL, 0)
            elif pr < NP_:
                by_col(0, BR, pr * BR - PADL)
            else:
                for i in range(6):
                    by_row(i, (HT - PADL + i) % HT)
            return parts

        NPART = [len(stage_parts(0, pr, 0, 9)) for pr in range(NP_ + 1)]
        CUM = [sum(NPART[:pr + 1]) for pr in range(NP_ + 1)]

        @block.sync
        def _(sp):
            for dst, src in ((w[:], w_out1), (bias[:], b_out1.partition_broadcast(1)),
                             (bl[:], b_ln.rearrange("c o -> o c"))):
                sp.dma_start(dst, src).then_inc(s_const, 16)

            def load_table(blk, k):
                sp.dma_start(wide[:, k], wide_d[blk].rearrange("p (c e) -> p c e", c=CB)).then_inc(s_t[k], 16)
                sp.dma_start(narrow[0:NARROW_K, k], narrow_d[blk].rearrange("p (c e) -> p c e", c=CB)
                             ).then_inc(s_t[k], 16)

            def load_rows(nth, img):
                sp.wait_ge(xl_done, nth * NST)
                sp.dma_start(nrow[:], norm_d[img].partition_broadcast(P)).then_inc(s_nrow, 16)

            def load_stage(nth, img, st):
                pr, hf = st // 2, st % 2
                sp.wait_ge(xl_done, nth * NST + max(st - 1, 0))
                for part, src in stage_parts(img, pr, *HQ[hf]):
                    sp.dma_start(stage[hf][part], src).then_inc(s_st[hf], 16)

            sp.wait_ge(s_chain, 1)
            for k in range(2):
                load_table(k, k)
            load_rows(0, 0)
            for st in range(NST):
                load_stage(0, 0, st)
            with sp.Fori(0, IMGS) as img:
                nxt = (img + 1) % IMGS
                with sp.Fori(0, NBLK // 2 - 1) as it:
                    for k in range(2):
                        blk = it * 2 + 2 + k
                        sp.wait_ge(conv_ready, img * NBLK + it * 2 + k + 1)
                        load_table(blk, k)
                load_rows(img + 1, nxt)
                load_stage(img + 1, nxt, 0)
                load_stage(img + 1, nxt, 1)
                sp.wait_ge(h_done, img * NGRP + NGRP)
                for r in range(BR + 2):
                    if r < BR:
                        k = r % RES
                        if r >= RES:
                            sp.wait_ge(s_out[k], 16 * (img * (BR // RES) + r // RES))
                        src = x1_d[img, r:HT:BR, PADL:PADL + WD, :].rearrange("p (q s) c -> p q (s c)", s=BC_)
                        sp.dma_start(res[:, k, :], src).then_inc(s_res[k], 16)
                        load_stage(img + 1, nxt, r + 2)
                    if r == BR - 4:
                        sp.wait_ge(conv_ready, img * NBLK + NBLK)
                        for k in range(2):
                            load_table(k, k)
                    if r >= 2:
                        m = r - 2
                        sp.wait_ge(s_added, img * BR + m + 1)
                        dst = out[img, m:HT:BR].rearrange("p (q s) c -> p q (s c)", s=BC_)
                        sp.dma_start(dst, res[:, m % RES, :]).then_inc(s_out[m % RES], 16)
            for k in range(RES):
                sp.wait_ge(s_out[k], 16 * IMGS * BR // RES)
            for k in range(2):
                sp.wait_ge(s_t[k], 32 * (IMGS * (NBLK // 2) + 1))

        def scale_stage(pool, nth, st):
            pr, hf = st // 2, st % 2
            np_ = P if pr < NP_ else NARROW_K
            if st == 0:
                pool.wait_ge(s_nrow, 16 * nth + 16)
            pool.wait_ge(s_st[hf], nth * (16 * CUM[-1]) + 16 * CUM[pr])
            v = stage[hf][0:np_]
            nc.gpsimd.tensor_tensor(v, v, nrow[0:np_, 0:1, :].to_broadcast([np_, HQ[hf][1], C]),
                                    ALU.mult).then_inc(s_scaled, 1)

        def shift_stage(dve, nth, st):
            pr, hf = st // 2, st % 2
            np_ = P if pr < NP_ else NARROW_K
            dve.wait_ge(s_scaled, nth * NST + st + 1)
            v = stage[hf][0:np_]
            nc.vector.tensor_tensor(v, v, nrow[0:np_, 1:2, :].to_broadcast([np_, HQ[hf][1], C]),
                                    ALU.add).then_inc(s_normed, 1)

        def high_stage(act, nth, st):
            pr, hf = st // 2, st % 2
            np_ = P if pr < NP_ else NARROW_K
            q0, nq = HQ[hf]
            act.wait_ge(s_normed, nth * NST + st + 1)
            nc.scalar.copy(xhl[0:np_, 0, pr, q0:q0 + nq, :], stage[hf][0:np_]).then_inc(xh_done, 1)

        def low_stage(dve, nth, st):
            pr, hf = st // 2, st % 2
            np_ = P if pr < NP_ else NARROW_K
            q0, nq = HQ[hf]
            dve.wait_ge(xh_done, nth * NST + st + 1)
            nc.vector.tensor_tensor(xhl[0:np_, 1, pr, q0:q0 + nq, :], stage[hf][0:np_], xhl[0:np_, 0, pr, q0:q0 + nq, :],
                                    ALU.subtract).then_inc(xl_done, 1)

        @block.gpsimd
        def _(pool):
            for st in range(NST):
                scale_stage(pool, 0, st)
            with pool.Fori(0, IMGS) as img:
                with pool.Fori(0, NBLK // 2) as it:
                    for k in range(2):
                        pool.wait_ge(xh_done, img * NST + NST)
                        pool.wait_ge(xl_done, img * NST + NST)
                        pool.wait_ge(s_prod[k], img * (NBLK // 2) + it)
                        cs = bass.ds(it * (2 * CB) + k * CB, CB)
                        dst = right[:, k].rearrange("p a (b q) c -> p (a b) q c", q=NQ)
                        src = xhl[:, :, :, :, cs].rearrange("p a b q c -> p (a b) q c")
                        nc.gpsimd.tensor_copy(dst[:, :, 0:NQ - 1, :], src[:, :, 1:NQ, :])
                        nc.gpsimd.tensor_copy(dst[:, :, NQ - 1, :], src[:, :, 0, :]).then_inc(s_right, 1)
                for st in range(NST):
                    scale_stage(pool, img + 1, st)

        @block.tensor
        def _(pe):
            pe.wait_ge(s_const, 48)
            pe.wait_ge(s_chain, 8)

            def conv_channel(k, ci, c):
                dst = psC[k][:, ci]
                n = 0
                for q, (dp, dq, r0, c0) in enumerate(QUADS):
                    tab = (wide if q < 2 else narrow)[:, k, ci, QBASE[q]:QBASE[q] + 4 * QSIZE[q]]
                    tab = tab.rearrange("p (a e) -> p a e", a=2)
                    if c0 == 0:
                        o = dst[:, :, r0 * BC_:]
                    elif r0 == 0:
                        o = dst.rearrange("p v (r s) -> p (v r) s", s=BC_)[:, :, c0:]
                    else:
                        o = dst.rearrange("p v (r s) -> p v r s", s=BC_)[:, :, r0:, c0:]
                    for hl, part in ((0, 0), (0, 1), (1, 0)):
                        if dq:
                            lhs = right[:, k, hl, dp * NQ:(dp + NP_) * NQ, ci]
                        else:
                            lhs = xhl[:, hl, dp:dp + NP_, :, bass.ds(c, 1)].rearrange("p a b c -> p (a b c)")
                        mm = nc.tensor.matmul(o, lhs, tab[:, part, :], start=(n == 0), stop=(n == 11))
                        n += 1
                return mm

            with pe.Fori(0, IMGS) as img:
                with pe.Fori(0, NBLK // 2) as it:
                    for k in range(2):
                        pe.wait_ge(s_t[k], img * (NBLK // 2 * 32) + it * 32 + 32)
                        pe.wait_ge(s_right, img * NBLK + it * 2 + k + 1)
                        pe.wait_ge(s_prod[k], img * (NBLK // 2) + it)
                        for ci in range(CB):
                            mm = conv_channel(k, ci, it * (2 * CB) + k * CB + ci)
                        mm.then_inc(conv_ready, 1)
                pe.wait_ge(h_done, img * NGRP + NGRP)
                for r in range(BR + 1):
                    if r < BR:
                        pe.wait_ge(ht_evac, img * BR + r)
                        for s in range(BC_):
                            mm = nc.tensor.transpose(psH[:, s, :], h[:, r * BC_ + s, :], ident[:])
                        mm.then_inc(ht_ready, 1)
                    if r >= 1:
                        m = r - 1
                        pe.wait_ge(ht_evac, img * BR + m + 1)
                        if m in FIX:
                            nfix = sum(1 for z in FIX if z <= m)
                            pe.wait_ge(s_fixed, img * KS + nfix)
                        pe.wait_ge(s_added, img * BR + m)
                        for b in range(2):
                            def add_bias(part):
                                return nc.tensor.matmul(
                                    psO[:, b * 512:(b + 1) * 512].rearrange("p (s c) -> p s c", c=C),
                                    ones3[:], bias3[:, part:part + 1, :].to_broadcast([1, 4, C]),
                                    start=(part == 0), stop=(part == 2))

                            add_bias(0)
                            add_bias(1)
                            for s in range(4 * b, 4 * b + 4):
                                nc.tensor.matmul(psO[:, s * C:(s + 1) * C], hT[:, m % 2, s * P:(s + 1) * P], w[:],
                                                 start=False, stop=False)
                            mm = add_bias(2)
                        mm.then_inc(o_ready, 1)

        @block.scalar
        def _(act):
            for st in range(NST):
                if st == 0:
                    act.wait_ge(s_chain, 2)
                high_stage(act, 0, st)
            with act.Fori(0, IMGS) as img:
                for g in range(NGRP):
                    for b in range(BPG):
                        blk = g * BPG + b
                        act.wait_ge(conv_ready, img * NBLK + blk + 1)
                        if blk == 0:
                            for k in range(RES):
                                act.wait_ge(s_out[k], 16 * (img * (BR // RES)))
                        if b == 0 and g >= 2:
                            act.wait_ge(h_done, img * NGRP + g - 1)
                        nc.scalar.activation(tbuf[:, g % 2, b * CB:(b + 1) * CB, :], psC[blk % 2][:, :, 1, :],
                                             ACT.Tanh, scale=0.5).then_inc(th_done, 1)
                    u = ubuf[:].rearrange("p g c -> p (g c)")
                    act.wait_ge(s_nabs, img * NGRP + g + 1)
                    nc.scalar.activation(u, u, ACT.Exp).then_inc(s_exp, 1)
                    act.wait_ge(s_exp, img * NGRP + g + 1)
                    nc.scalar.activation(u, u, ACT.Ln, bias=1.0).then_inc(s_ln, 1)
                act.wait_ge(conv_ready, img * NBLK + NBLK)
                for r in range(NST):
                    if r < BR:
                        act.wait_ge(ht_ready, img * BR + r + 1)
                        act.wait_ge(o_ready, img * BR + max(r - 1, 0))
                        nc.scalar.activation(hT[:, r % 2, :], psH[:].rearrange("p s c -> p (s c)"), ACT.Copy,
                                             bias=A_FREE * H_EPS, scale=A_FREE).then_inc(ht_evac, 1)
                    high_stage(act, img + 1, r)

        @block.vector
        def _(dve):
            t = Tally(dve, s_chain)
            t.then(nc.vector.memset(narrow[:].rearrange("p a c e -> p (a c e)"), 0.0))
            for a in range(2):
                t.then(nc.vector.memset(xhl[:, a, NP_].rearrange("p q c -> p (q c)"), 0.0))
            t.then(nc.vector.memset(ones3[:], 1.0))
            dve.wait_ge(s_const, 48)
            t.then(nc.vector.tensor_tensor(bias[:], bias[:], bl[:], ALU.add))
            for i in range(3):
                ins = nc.vector.tensor_copy(bias3[:, i, :], bias[:])
                if i == 2:
                    t.then(ins)
                else:
                    ins.then_inc(s_bias, 1)
                    dve.wait_ge(s_bias, i + 1)
                    t.then(nc.vector.tensor_tensor(bias[:], bias[:], bias3[:, i, :], ALU.subtract))
            for st in range(NST):
                shift_stage(dve, 0, st)
                low_stage(dve, 0, st)

            def product(img, g, b):
                blk = g * BPG + b
                dve.wait_ge(th_done, img * NBLK + blk + 1)
                tb = tbuf[:, g % 2, b * CB:(b + 1) * CB, :]
                nc.vector.scalar_tensor_tensor(tb, tb, 1.0, psC[blk % 2][:, :, 0, :], ALU.add, ALU.mult
                                               ).then_inc(s_prod[blk % 2], 1)

            def negative_abs(img, g):
                for k in range(2):
                    dve.wait_ge(s_prod[k], img * (NBLK // 2) + (g + 1) * (BPG // 2))
                tb = tbuf[:, g % 2].rearrange("p g c -> p (g c)")
                nc.vector.scalar_tensor_tensor(ubuf[:].rearrange("p g c -> p (g c)"), tb, -1.0, tb,
                                               ALU.mult, ALU.min).then_inc(s_nabs, 1)

            def softplus(img, g):
                dve.wait_ge(s_ln, img * NGRP + g + 1)
                hv = h[:, :, g * GCH:(g + 1) * GCH].rearrange("p o c -> p c o")
                nc.vector.scalar_tensor_tensor(hv, tbuf[:, g % 2], 0.0, ubuf[:], ALU.max, ALU.add
                                               ).then_inc(h_done, 1)

            with dve.Fori(0, IMGS) as img:
                for g in range(NGRP):
                    product(img, g, 0)
                    product(img, g, 1)
                    if g >= 1:
                        softplus(img, g - 1)
                    product(img, g, 2)
                    product(img, g, 3)
                    negative_abs(img, g)
                softplus(img, NGRP - 1)
                nfix = 0
                for r in range(NST):
                    shift_stage(dve, img + 1, r)
                    if r in FIX:
                        pr, yy = FIX[r]
                        dve.wait_ge(ht_evac, img * BR + r + 1)
                        cor = corner[:, yy, :, bass.ds(img, 1)].squeeze(2)
                        last = hT[:, r % 2, 5 * P + pr * NQ + NQ - 1:8 * P:P]
                        first = hT[:, r % 2, pr * NQ:4 * P:P]
                        nc.vector.tensor_tensor(last, last, cor[:, 0:3], ALU.mult)
                        nc.vector.tensor_tensor(first, first, cor[:, 3:7], ALU.mult).then_inc(s_fixed, 1)
                    if r < BR:
                        k = r % RES
                        dve.wait_ge(o_ready, img * BR + r + 1)
                        dve.wait_ge(s_res[k], 16 * (img * (BR // RES) + r // RES + 1))
                        nc.vector.tensor_tensor(res[:, k, :], psO[:], res[:, k, :], ALU.add).then_inc(s_added, 1)
                    low_stage(dve, img + 1, r)


def kernel(x, L0_conv_w_qkv, L0_conv_w_out, L0_conv_b_out, L0_conv_g_ln, L0_conv_b_ln, L1_conv_A_kernel,
           L1_conv_B_kernel, L1_conv_gate_A_kernel, L1_conv_gate_B_kernel, L1_conv_W_out, L1_conv_b_out):
    import concourse.bacc as bacc
    from concourse.bass_utils import run_bass_kernel_spmd

    f = lambda a: np.ascontiguousarray(np.asarray(a))
    taps_first = lambda k: np.ascontiguousarray(np.asarray(k).reshape(C, TAPS).T)
    arrays = {
        "x": f(x).reshape(IMGS, N, C),
        "w_qkv": f(L0_conv_w_qkv), "w_out0": f(L0_conv_w_out), "b_out0": f(L0_conv_b_out),
        "g_ln": f(L0_conv_g_ln).reshape(C), "b_ln": f(L0_conv_b_ln).reshape(C, 1),
        "kB": taps_first(L1_conv_B_kernel), "kGB": taps_first(L1_conv_gate_B_kernel),
        "kA": f(L1_conv_A_kernel).reshape(C, TAPS), "kGA": f(L1_conv_gate_A_kernel).reshape(C, TAPS),
        "w_out1": f(L1_conv_W_out), "b_out1": f(L1_conv_b_out),
        "ident": np.eye(P, dtype=np.float32),
        "group": np.kron(np.eye(C // GROUP), np.full((GROUP, GROUP), 1.0 / (GROUP * N))).astype(np.float32),
        "head": np.kron(np.eye(HEADS), np.full((DH, DH), DH ** -0.5)).astype(np.float32),
        "sel": selection_table(),
    }
    nc = bacc.Bacc("TRN2", target_bir_lowering=False, num_devices=1)
    args = [nc.dram_tensor("in_" + k, a.shape, mybir.dt.from_np(a.dtype), kind="ExternalInput").ap()
            for k, a in arrays.items()]
    out = nc.dram_tensor("out", (IMGS, HT, WD, C), F32, kind="ExternalOutput").ap()
    build(nc, *args, out)
    r = run_bass_kernel_spmd(nc, [{"in_" + k: a for k, a in arrays.items()}], core_ids=[0])
    return r.results[0]["out"]
```

```python
from contextlib import ExitStack

import numpy as np

import concourse.bass as bass
from concourse import mybir

F32 = mybir.dt.float32
BF16 = mybir.dt.bfloat16
ALU = mybir.AluOpType
ACT = mybir.ActivationFunctionType
AX = mybir.AxisListType

P = 128
IMGS, HT, WD, C = 16, 128, 128, 128
N = HT * WD
HEADS, DH = 4, 32
GROUP = 4
GN_EPS, LN_EPS, H_EPS = 1e-5, 1e-5, 1e-6
KS = 7
TAPS = KS * KS
STEPS = 8
A_FREE = 1.0 - 0.5 ** STEPS

TPC = 8
CT = TPC * P
NCH = N // CT
ROWS_CH = CT // WD

STAT_T = 16
STAT_CH = N // (STAT_T * P)
STAT_RING = 4

BR, BC_ = 16, 8
NP_, NQ = HT // BR, WD // BC_
PADL = 3

QUADS = [(0, 0, 0, 0), (0, 1, 0, 2), (1, 0, 10, 0), (1, 1, 10, 2)]
QSIZE = [(BR - r0) * (BC_ - c0) for _, _, r0, c0 in QUADS]
QBASE = [0, 4 * QSIZE[0], 0, 4 * QSIZE[2]]
WIDE = 4 * (QSIZE[0] + QSIZE[1])
NARROW = 4 * (QSIZE[2] + QSIZE[3])
NARROW_K = 6 * BC_
CB = 4
NBLK = C // CB
TC = 2
TRING = 4
GCH = 16
NGRP = C // GCH
BPG = GCH // CB
ZI, ZJ = 2 * BR + 5, 2 * BC_ + 5


def selection_table():
    z = np.zeros((KS, KS, ZI, ZJ), np.float32)
    for u in range(KS):
        for v in range(KS):
            z[u, v, 21 - u, 13 - v] = 1.0
    table = np.zeros((P, ZI * ZJ), np.float32)
    table[:TAPS] = z.reshape(TAPS, ZI * ZJ)
    return table


def build(nc, x, w_qkv, w_out0, b_out0, g_ln, b_ln, kB, kGB, kA, kGA, w_out1, b_out1,
          ident_d, group_d, head_d, sel_d, out):
    x1_d = nc.dram_tensor("x1_scratch", (IMGS, NQ + 1, HT, BC_, C), F32).ap()
    wide_d = nc.dram_tensor("toeplitz_wide", (C // TC, P, TC * WIDE), BF16).ap()
    narrow_d = nc.dram_tensor("toeplitz_narrow", (C // TC, NARROW_K, TC * NARROW), BF16).ap()
    norm_d = nc.dram_tensor("norm_rows", (IMGS, 2, C), F32).ap()

    with ExitStack() as whole:
        def keep(name, shape, dt=F32):
            return whole.enter_context(nc.sbuf_tensor(name, shape, dt))

        ident = keep("ident", [P, P])
        group = keep("group", [P, P])
        bln_col = keep("bln_col", [P, 1])
        scale1 = keep("scale1", [P, IMGS])
        shift1 = keep("shift1", [P, IMGS])
        scale2 = keep("scale2", [P, IMGS])
        shift2 = keep("shift2", [P, IMGS])
        sums2 = keep("sums2", [P, 2, IMGS])
        corner = keep("corner", [P, KS, KS, IMGS])

        setup(nc, x, kB, kGB, ident_d, group_d, sel_d, b_ln, wide_d, narrow_d,
              ident, group, bln_col, scale1, shift1)
        layer0(nc, x, w_qkv, w_out0, b_out0, g_ln, head_d, x1_d, ident, scale1, shift1, sums2)
        corner_block(nc, kA, kGA, x1_d, norm_d, ident, group, bln_col, sums2, scale2, shift2, corner)
        layer1(nc, w_out1, b_out1, b_ln, x1_d, wide_d, narrow_d, norm_d, ident, corner, out)


class Tally:

    def __init__(self, eng, sem):
        self.eng, self.sem, self.n = eng, sem, 0

    def then(self, ins):
        ins.then_inc(self.sem, 1)
        self.n += 1
        self.eng.wait_ge(self.sem, self.n)


def setup(nc, x, kB, kGB, ident_d, group_d, sel_d, b_ln, wide_d, narrow_d,
          ident, group, bln_col, scale1, shift1):
    NB = BR * 2 + 6 * 2
    BANKS = 4
    TPG = GCH // TC
    with ExitStack() as ctx:
        sb = lambda n, s, d=F32: ctx.enter_context(nc.sbuf_tensor(n, s, d))
        ps = lambda n, s, d=F32: ctx.enter_context(nc.psum_tensor(n, s, d))
        sem = lambda n: ctx.enter_context(nc.semaphore(n))
        xs = sb("stat_x", [P, STAT_RING, STAT_T * C])
        sq = sb("stat_sq", [P, 2, STAT_T * C])
        accx = sb("accx", [P, STAT_T * C])
        accs = sb("accs", [P, STAT_T * C])
        red = sb("red", [P, 2, C])
        ones = sb("stat_ones", [P, 1])
        self32 = sb("sel_f32", [P, ZI * ZJ])
        sel = sb("sel", [P, 14, ZI, BC_], BF16)
        taps = sb("taps", [P, 2, C])
        tap_hl = sb("tap_hl", [P, 4, C], BF16)
        table = sb("table", [P, GCH, WIDE + NARROW], BF16)
        sums = sb("sums1", [P, 2, IMGS])
        stat = sb("stat1", [P, 2, IMGS])
        var = sb("var1", [P, IMGS])
        half = sb("minus_half1", [P, IMGS])
        psT = [ps(f"psT{k}", [P, 512]) for k in range(BANKS)]
        psS = [ps(f"psS{k}", [P, 512]) for k in range(2)]
        psG = ps("psG1", [P, 512])

        s_const = sem("a_const")
        s_dve = sem("a_dve")
        s_ready = sem("a_taps_ready")
        s_trow = sem("a_table_row")
        s_tfree = [sem(f"a_table_bank_free{k}") for k in range(BANKS)]
        s_tstored = sem("a_table_stored")
        s_x = [sem(f"a_x_loaded{k}") for k in range(STAT_RING)]
        s_xdve = sem("a_x_added_dve")
        s_xpool = sem("a_x_added_pool")
        s_accs = sem("a_squares_added")
        s_red = sem("a_reduced")
        s_summed = sem("a_summed")
        s_sq = sem("a_sq_ready")
        s_sums = sem("a_sums_done")
        s_group = sem("a_group")
        s_stat = sem("a_stat")
        s_pow = sem("a_pow")
        block = ctx.enter_context(nc.Block())
        NCONST = 6
        HALF = STAT_T * C // 2

        rows = []
        for q, (dp, dq, r0, c0) in enumerate(QUADS):
            for r in range(r0, BR):
                rows.append((q, dp, dq, r, c0, (r - r0) * (BC_ - c0)))
        assert len(rows) == NB

        def evac(eng_copy, j, k):
            q, dp, dq, r, c0, off = rows[j]
            ns = BC_ - c0
            base = QBASE[q] if q < 2 else WIDE + QBASE[q]
            src = psT[k][:, 0:ns * 4 * GCH].rearrange("p (s m c) -> p c m s", m=4, c=GCH)
            dst = table[:, :, base:base + 4 * QSIZE[q]].rearrange("p c (m o) -> p c m o", m=4)[:, :, :, off:off + ns]
            return eng_copy(dst, src)

        @block.sync
        def _(sp):
            sp.wait_ge(s_dve, 1)
            for dst, src in ((ident[:], ident_d), (group[:], group_d), (self32[:], sel_d),
                             (taps[0:TAPS, 0, :], kB), (taps[0:TAPS, 1, :], kGB), (bln_col[:], b_ln)):
                sp.dma_start(dst, src).then_inc(s_const, 16)
            with sp.Fori(0, NGRP) as g:
                for k in range(BANKS):
                    sp.wait_ge(s_tfree[k], (g + 1) * (NB // BANKS))
                for b in range(TPG):
                    sp.dma_start(wide_d[g * TPG + b].rearrange("p (c e) -> p c e", c=TC),
                                 table[:, b * TC:(b + 1) * TC, 0:WIDE]).then_inc(s_tstored, 16)
                    sp.dma_start(narrow_d[g * TPG + b].rearrange("p (c e) -> p c e", c=TC),
                                 table[0:NARROW_K, b * TC:(b + 1) * TC, WIDE:WIDE + NARROW]
                                 ).then_inc(s_tstored, 16)
            sp.wait_ge(s_tstored, NGRP * TPG * 32)
            def load(img, n):
                src = x[img].rearrange("(n p t) c -> n p (t c)", p=P, t=STAT_T)[n]
                sp.dma_start(xs[:, n % STAT_RING, :], src).then_inc(s_x[n % STAT_RING], 16)

            def slot_free(img, n):
                for s in (s_sq, s_xdve, s_xpool):
                    sp.wait_ge(s, img * STAT_CH + n + 1)

            for n in range(STAT_RING):
                load(0, n)
            with sp.Fori(0, IMGS - 1) as img:
                for n in range(STAT_CH):
                    slot_free(img, n)
                    load(img + (n + STAT_RING) // STAT_CH, (n + STAT_RING) % STAT_CH)
            for n in range(STAT_CH - STAT_RING):
                slot_free(IMGS - 1, n)
                load(IMGS - 1, n + STAT_RING)

        @block.gpsimd
        def _(pool):
            with pool.Fori(0, IMGS) as img:
                for n in range(STAT_CH):
                    pool.wait_ge(s_x[n % STAT_RING], 16 * (img * (STAT_CH // STAT_RING) + n // STAT_RING + 1))
                    src = xs[:, n % STAT_RING, 0:HALF]
                    if n == 1:
                        pool.wait_ge(s_red, img)
                        nc.gpsimd.tensor_tensor(accx[:, 0:HALF], xs[:, 0, 0:HALF], src, ALU.add).then_inc(s_xpool, 2)
                    elif n > 1:
                        pool.wait_ge(s_xpool, img * STAT_CH + n)
                        nc.gpsimd.tensor_tensor(accx[:, 0:HALF], accx[:, 0:HALF], src, ALU.add).then_inc(s_xpool, 1)
            nc.gpsimd.memset(half[:], -0.5).then_inc(s_pow, 1)
            pool.wait_ge(s_pow, 1)
            pool.wait_ge(s_stat, 2)
            nc.gpsimd.tensor_tensor(scale1[:], var[:], half[:], ALU.pow).then_inc(s_pow, 1)

        @block.tensor
        def _(pe):
            pe.wait_ge(s_ready, 1)
            with pe.Fori(0, NGRP) as g:
                for j, (q, dp, dq, r, c0, off) in enumerate(rows):
                    k = j % BANKS
                    pe.wait_ge(s_tfree[k], g * (NB // BANKS) + j // BANKS)
                    i0 = 21 - (r + 6 - BR * dp)
                    for s in range(c0, BC_):
                        j0 = 13 - (s + 6 - BC_ * dq)
                        mm = nc.tensor.matmul(
                            psT[k][:, (s - c0) * 4 * GCH:(s - c0 + 1) * 4 * GCH],
                            sel[:, j0, i0:i0 + BR, :].rearrange("t i j -> t (i j)"), tap_hl[:, :, bass.ds(g * GCH, GCH)],
                            start=True, stop=True)
                    mm.then_inc(s_trow, 1)
            with pe.Fori(0, IMGS) as img:
                pe.wait_ge(s_red, img + 1)
                pe.wait_ge(s_sums, img)
                for a in range(2):
                    mm = nc.tensor.matmul(psS[a][:, 0:1], red[:, a, :], ones[:], start=True, stop=True)
                mm.then_inc(s_summed, 1)
            pe.wait_ge(s_sums, IMGS)
            nc.tensor.matmul(psG[:, 0:2 * IMGS], group[:], sums[:].rearrange("p a b -> p (a b)"),
                             start=True, stop=True).then_inc(s_group, 1)

        @block.scalar
        def _(act):
            with act.Fori(0, NGRP) as g:
                for j in range(1, NB, 2):
                    act.wait_ge(s_trow, g * NB + j + 1)
                    if j == 1:
                        act.wait_ge(s_tstored, g * (TPG * 32))
                    evac(nc.scalar.copy, j, j % BANKS).then_inc(s_tfree[j % BANKS], 1)
            with act.Fori(0, IMGS) as img:
                for n in range(STAT_CH):
                    k = n % STAT_RING
                    act.wait_ge(s_x[k], 16 * (img * (STAT_CH // STAT_RING) + n // STAT_RING + 1))
                    if n == 0:
                        act.wait_ge(s_red, img)
                        dst = accs[:]
                    else:
                        act.wait_ge(s_accs, img * (STAT_CH - 1) + max(n - 2, 0))
                        dst = sq[:, n % 2, :]
                    nc.scalar.activation(dst, xs[:, k, :], ACT.Square).then_inc(s_sq, 1)

        @block.vector
        def _(dve):
            t = Tally(dve, s_dve)
            t.then(nc.vector.memset(taps[:], 0.0))
            t.then(nc.vector.memset(ones[:], 1.0))
            dve.wait_ge(s_const, 16 * NCONST)
            for j0 in range(14):
                t.then(nc.vector.tensor_copy(sel[:, j0], self32[:].rearrange("t (a b) -> t a b", b=ZJ)[:, :, j0:j0 + BC_]))
            t.then(nc.vector.tensor_scalar(taps[:, 0, :], taps[:, 0, :], 0.5, None, ALU.mult))
            t.then(nc.vector.tensor_copy(tap_hl[:, 0:2, :], taps[:]))
            nc.vector.tensor_tensor(tap_hl[:, 2:4, :], taps[:], tap_hl[:, 0:2, :],
                                    ALU.subtract).then_inc(s_ready, 1)
            with dve.Fori(0, NGRP) as g:
                for j in range(0, NB, 2):
                    dve.wait_ge(s_trow, g * NB + j + 1)
                    if j == 0:
                        dve.wait_ge(s_tstored, g * (TPG * 32))
                    evac(nc.vector.tensor_copy, j, j % BANKS).then_inc(s_tfree[j % BANKS], 1)
            with dve.Fori(0, IMGS) as img:
                for n in range(STAT_CH):
                    dve.wait_ge(s_x[n % STAT_RING], 16 * (img * (STAT_CH // STAT_RING) + n // STAT_RING + 1))
                    src = xs[:, n % STAT_RING, HALF:]
                    if n == 0:
                        ins = nc.vector.tensor_copy(accx[:, HALF:], src)
                    else:
                        dve.wait_ge(s_xdve, img * STAT_CH + n)
                        ins = nc.vector.tensor_tensor(accx[:, HALF:], accx[:, HALF:], src, ALU.add)
                    ins.then_inc(s_xdve, 1)
                    if n:
                        dve.wait_ge(s_sq, img * STAT_CH + n + 1)
                        dve.wait_ge(s_accs, img * (STAT_CH - 1) + n - 1)
                        nc.vector.tensor_tensor(accs[:], accs[:], sq[:, n % 2, :], ALU.add).then_inc(s_accs, 1)
                dve.wait_ge(s_xdve, (img + 1) * STAT_CH)
                dve.wait_ge(s_xpool, (img + 1) * STAT_CH)
                dve.wait_ge(s_accs, (img + 1) * (STAT_CH - 1))
                dve.wait_ge(s_summed, img)
                nc.vector.tensor_reduce(red[:, 0, :], accx[:].rearrange("p (t c) -> p c t", c=C), AX.X, ALU.add)
                nc.vector.tensor_reduce(red[:, 1, :], accs[:].rearrange("p (t c) -> p c t", c=C), AX.X, ALU.add
                                        ).then_inc(s_red, 1)
                dve.wait_ge(s_summed, img + 1)
                nc.vector.tensor_copy(sums[:, 0, bass.ds(img, 1)], psS[0][:, 0:1])
                nc.vector.tensor_copy(sums[:, 1, bass.ds(img, 1)], psS[1][:, 0:1]).then_inc(s_sums, 1)
            dve.wait_ge(s_group, 1)
            norm_scale(nc, dve, t, psG, stat, var, s_stat)
            dve.wait_ge(s_pow, 2)
            t.then(nc.vector.scalar_tensor_tensor(shift1[:], stat[:, 0, :], -1.0, scale1[:],
                                                  ALU.mult, ALU.mult))


def norm_scale(nc, dve, t, psG, stat, var, s_stat):
    t.then(nc.vector.tensor_copy(stat[:].rearrange("p a b -> p (a b)"), psG[:, 0:2 * IMGS]))
    t.then(nc.vector.tensor_tensor(var[:], stat[:, 0, :], stat[:, 0, :], ALU.mult))
    ins = nc.vector.tensor_tensor(var[:], stat[:, 1, :], var[:], ALU.subtract)
    ins.then_inc(s_stat, 1)
    dve.wait_ge(s_stat, 1)
    nc.vector.tensor_scalar(var[:], var[:], 0.0, GN_EPS, ALU.max, ALU.add).then_inc(s_stat, 1)
    dve.wait_ge(s_stat, 2)


def layer0(nc, x, w_qkv, w_out0, b_out0, g_ln, head_d, x1_d, ident, scale1, shift1, sums2):
    with ExitStack() as ctx:
        sb = lambda n, s, d=F32: ctx.enter_context(nc.sbuf_tensor(n, s, d))
        ps = lambda n, s, d=F32: ctx.enter_context(nc.psum_tensor(n, s, d))
        sem = lambda n: ctx.enter_context(nc.semaphore(n))
        X = [sb(f"X{n}", [P, TPC, C]) for n in range(NCH)]
        gT = [sb(f"gT{k}", [C, CT]) for k in range(2)]
        ekT = [sb(f"ekT{k}", [P, CT]) for k in range(2)]
        ek = [sb(f"ek{k}", [P, TPC, P]) for k in range(2)]
        q = [sb(f"q{k}", [P, TPC, P]) for k in range(3)]
        qT = sb("qT", [P, CT])
        sqo = sb("sqo", [P, TPC, C])
        y = [sb(f"y{k}", [P, TPC, C]) for k in range(2)]
        sqx = [sb(f"sqx{k}", [P, TPC, C]) for k in range(2)]
        wqkv = sb("wqkv", [C, 3 * C])
        head = sb("head", [P, P])
        wo = sb("wo", [P, 2, C])
        brow = sb("brow", [P, 2, C])
        grow = sb("grow", [P, C])
        mean_w = sb("mean_w", [P, 2])
        ones = sb("ones0", [P, 1])
        nmax = sb("nmax", [P, NCH + 1])
        nmax_c = sb("nmax_c", [P, NCH])
        corr = sb("corr", [P, NCH])
        ksum_c = sb("ksum_c", [P, NCH])
        ksum = sb("ksum", [P, NCH + 1])
        acc = sb("acc", [P, C])
        accn = sb("accn", [P, C])
        ctxg = sb("ctxg", [C, P])
        ctxT = sb("ctxT", [P, P])
        M = sb("M", [P, 2, C])
        rk = sb("rk", [P, 1])
        qmax = sb("qmax", [P, 3, TPC * HEADS])
        qsum = sb("qsum", [P, 3, TPC * HEADS])
        qinv = sb("qinv", [P, 3, TPC * HEADS])
        vsum = sb("vsum", [P, 2, TPC])
        rstd = sb("rstd", [P, 2, TPC])
        half = sb("minus_half0", [P, TPC])
        ceps = sb("ceps", [P, TPC])
        norm = sb("norm0", [P, 2])
        accx = sb("accx0", [P, TPC, C])
        accs = sb("accs0", [P, TPC, C])
        red = sb("red0", [P, 2, C])
        psX = ps("psX", [P, CT])
        psK = ps("psK", [P, CT])
        psW = ps("psW", [P, 2 * CT])

        s_const = sem("b_const")
        s_chain = sem("b_chain")
        s_x = [sem(f"b_x_loaded{n}") for n in range(NCH)]
        s_store = [sem(f"b_stored{n}") for n in range(NCH)]
        psx_ready = sem("b_psx_ready")
        psx_drained = sem("b_psx_drained")
        psk_ready = sem("b_psk_ready")
        k_exped = sem("b_k_exped")
        q_subbed = sem("b_q_subbed")
        s_nmc = sem("b_nmc")
        s_nmax = sem("b_nmax")
        s_corr = sem("b_corr")
        et_ready = sem("b_et_ready")
        ek_ready = sem("b_ek_ready")
        ctx_done = sem("b_ctx_done")
        acc_done = sem("b_acc_done")
        s_m = sem("b_m_steps")
        s_qmax = sem("b_qmax")
        s_qexp = sem("b_qexp")
        s_qsum = sem("b_qsum")
        s_qinv = sem("b_qinv")
        s_qn = sem("b_qn")
        o_ready = sem("b_o_ready")
        s_sqo = sem("b_sqo")
        s_vsum = sem("b_vsum")
        s_rstd1 = sem("b_rstd_a")
        s_rstd = sem("b_rstd")
        s_yraw = sem("b_y_raw")
        s_y = sem("b_y")
        s_x1 = sem("b_x1")
        s_sqx = sem("b_sqx")
        s_accx = sem("b_accx")
        s_accx_dve = sem("b_accx_dve")
        s_accs = sem("b_accs")
        s_red = sem("b_red")
        st_ready = sem("b_st_ready")
        st_taken = sem("b_st_taken")
        s_centred = sem("b_centred")
        s_half = sem("b_half")
        s_norm = sem("b_norm")
        s_mready = sem("b_m_ready")
        block = ctx.enter_context(nc.Block())
        NCONST = 5
        ACUT = TPC * 3 // 4

        B_SLOTS, C_SLOTS = NCH + 2, NCH + 7
        seqT, seqQ, seq = {}, {}, 0
        for n in range(NCH):
            seqT[("k", n)] = seq
            seq += 1
        for n in range(C_SLOTS):
            if 0 <= n - 3 < NCH:
                seqQ[n - 3] = seq
                seq += 1
            if n < NCH:
                seqT[("q", n)] = seq
                seq += 1
        SEQ = seq

        def x_chunk(img, n):
            return x[img].rearrange("(n p t) c -> n p t c", p=P, t=TPC)[n]

        @block.sync
        def _(sp):
            for dst, src in ((wqkv[:], w_qkv), (head[:], head_d), (wo[:, 0, :], w_out0),
                             (brow[:, 0, :], b_out0.partition_broadcast(P)),
                             (grow[:], g_ln.partition_broadcast(P))):
                sp.dma_start(dst, src).then_inc(s_const, 16)
            for n in range(NCH):
                sp.dma_start(X[n][:], x_chunk(0, n)).then_inc(s_x[n], 16)

            def reload(img, n):
                sp.wait_ge(s_store[n], 48 * (img + 1))
                sp.wait_ge(s_sqx, img * NCH + n + 1)
                sp.wait_ge(s_accx, img * NCH + n + 1)
                sp.wait_ge(s_accx_dve, img * NCH + n + 1)
                sp.dma_start(X[n][:], x_chunk(img + 1, n)).then_inc(s_x[n], 16)

            def image(img, last):
                for n in range(NCH):
                    sp.wait_ge(s_x1, img * NCH + n + 1)
                    rows = x1_d[img, :, ROWS_CH * n:ROWS_CH * (n + 1)].rearrange("q h j c -> h q (j c)")
                    flat = X[n][:].rearrange("p t c -> p (t c)")
                    cut = (TPC - PADL) * C
                    sp.dma_start(rows[:, 0:NQ, PADL * C:], flat[:, 0:cut]).then_inc(s_store[n], 16)
                    sp.dma_start(rows[:, 1:NQ + 1, 0:PADL * C], flat[:, cut:]).then_inc(s_store[n], 16)
                    sp.dma_start(rows[:, 0, 0:PADL * C], flat[15:P:16, cut:]).then_inc(s_store[n], 16)
                    if not last and n >= 4:
                        reload(img, n - 4)
                if not last:
                    for n in range(NCH - 4, NCH):
                        reload(img, n)

            with sp.Fori(0, IMGS - 1) as img:
                image(img, False)
            image(IMGS - 1, True)
            for n in range(NCH):
                sp.wait_ge(s_store[n], 48 * IMGS)

        @block.tensor
        def _(pe):
            pe.wait_ge(s_const, 16 * NCONST)
            pe.wait_ge(s_chain, 10)

            def fill_psx(img, tiles, seq):
                pe.wait_ge(psx_drained, img * SEQ + seq)
                for t in range(TPC):
                    mm = nc.tensor.transpose(psX[:, t * P:(t + 1) * P], tiles(t), ident[:])
                mm.then_inc(psx_ready, 1)

            def turn_x(img, n, phase):
                pe.wait_ge(s_x[n], 16 * img + 16)
                fill_psx(img, lambda t: X[n][:, t, :], seqT[(phase, n)])

            def keys(img, n):
                pe.wait_ge(psx_drained, img * SEQ + seqT[("k", n)] + 1)
                if n == 0:
                    pe.wait_ge(q_subbed, img * NCH)
                else:
                    pe.wait_ge(k_exped, img * NCH + n)
                for hf in range(2):
                    mm = nc.tensor.matmul(psK[:, hf * 512:(hf + 1) * 512], wqkv[:, C:2 * C],
                                          gT[n % 2][:, hf * 512:(hf + 1) * 512], start=True, stop=True)
                mm.then_inc(psk_ready, 1)

            def turn_ek(img, n):
                pe.wait_ge(k_exped, img * NCH + n + 1)
                if n == 0:
                    pe.wait_ge(s_yraw, img * NCH)
                pe.wait_ge(ek_ready, img * NCH + n)
                for t in range(TPC):
                    mm = nc.tensor.transpose(psW[:, t * P:(t + 1) * P], ekT[n % 2][:, t * P:(t + 1) * P], ident[:])
                mm.then_inc(et_ready, 1)

            def context(img, n):
                pe.wait_ge(ek_ready, img * NCH + n + 1)
                pe.wait_ge(acc_done, img * NCH + max(n - 1, 0))
                for t in range(TPC):
                    mm = nc.tensor.matmul(psW[:, CT + 512 * (n % 2):CT + 512 * (n % 2) + C], ek[n % 2][:, t, :],
                                          X[n][:, t, :], start=(t == 0), stop=(t == TPC - 1))
                mm.then_inc(ctx_done, 1)

            def queries(img, n):
                pe.wait_ge(psx_drained, img * SEQ + seqT[("q", n)] + 1)
                if n == 0:
                    pe.wait_ge(k_exped, img * NCH + NCH)
                else:
                    pe.wait_ge(q_subbed, img * NCH + n)
                for t in range(TPC):
                    mm = nc.tensor.matmul(psK[:, t * P:(t + 1) * P], gT[n % 2][:, t * P:(t + 1) * P],
                                          wqkv[:, 0:C], start=True, stop=True)
                mm.then_inc(psk_ready, 1)

            def turn_q(img, n):
                pe.wait_ge(s_qn, img * NCH + n + 1)
                fill_psx(img, lambda t: q[n % 3][:, t, :], seqQ[n])

            def project(img, n):
                pe.wait_ge(psx_drained, img * SEQ + seqQ[n] + 1)
                pe.wait_ge(s_yraw, img * NCH + n)
                for t in range(TPC):
                    mm = nc.tensor.matmul(psW[:, t * 2 * C:(t + 1) * 2 * C], qT[:, t * P:(t + 1) * P],
                                          M[:].rearrange("p a c -> p (a c)"), start=True, stop=True)
                mm.then_inc(o_ready, 1)

            def sums(img):
                pe.wait_ge(psx_drained, img * SEQ + SEQ)
                pe.wait_ge(s_red, img + 1)
                for a in range(2):
                    mm = nc.tensor.matmul(psX[:, 512 * a:512 * a + 1], red[:, a, :], ones[:], start=True, stop=True)
                mm.then_inc(st_ready, 1)

            with pe.Fori(0, IMGS) as img:
                for n in range(B_SLOTS):
                    if 0 <= n - 1 < NCH:
                        keys(img, n - 1)
                    if n < NCH:
                        if n == 0:
                            pe.wait_ge(st_taken, img)
                        turn_x(img, n, "k")
                    if 0 <= n - 2 < NCH:
                        context(img, n - 2)
                    if 0 <= n - 1 < NCH:
                        turn_ek(img, n - 1)
                pe.wait_ge(s_m, img * 7 + 2)
                nc.tensor.transpose(psW[:, 0:P], accn[:], ident[:]).then_inc(s_m, 1)
                pe.wait_ge(s_m, img * 7 + 4)
                nc.tensor.matmul(psW[:, 512:512 + P], wqkv[:, 2 * C:3 * C], ctxg[:], start=True, stop=True
                                 ).then_inc(s_m, 1)
                pe.wait_ge(s_m, img * 7 + 6)
                nc.tensor.matmul(psW[:, 1024:1024 + 2 * C], ctxT[:], wo[:].rearrange("p a c -> p (a c)"),
                                 start=True, stop=True).then_inc(s_m, 1)
                for n in range(C_SLOTS):
                    if 0 <= n - 3 < NCH:
                        turn_q(img, n - 3)
                    if 0 <= n - 1 < NCH:
                        queries(img, n - 1)
                    if n < NCH:
                        turn_x(img, n, "q")
                    if 0 <= n - 3 < NCH:
                        if n == 3:
                            pe.wait_ge(s_mready, img + 1)
                        project(img, n - 3)
                sums(img)

        @block.scalar
        def _(act):
            def norm_out(img, n, phase, g):
                act.wait_ge(psx_ready, img * SEQ + seqT[(phase, n)] + 1)
                act.wait_ge(psk_ready, img * 2 * NCH + max(g - 1, 0))
                nc.scalar.activation(gT[n % 2][:], psX[:], ACT.Identity, bias=norm[:, 1:2],
                                     scale=norm[:, 0:1]).then_inc(psx_drained, 1)

            def exp_k(img, n):
                act.wait_ge(s_nmax, img * NCH + n + 1)
                act.wait_ge(et_ready, img * NCH + max(n - 1, 0))
                nc.scalar.activation(ekT[n % 2][:], psK[:], ACT.Exp, bias=nmax[:, n + 1:n + 2],
                                     accum_out=ksum_c[:, n:n + 1]).then_inc(k_exped, 1)
                nc.scalar.activation(corr[:, n:n + 1], nmax[:, n:n + 1], ACT.Exp, bias=nmax[:, n + 1:n + 2],
                                     scale=-1.0).then_inc(s_corr, 1)

            with act.Fori(0, IMGS) as img:
                act.wait_ge(s_norm, img + 1)
                for n in range(B_SLOTS):
                    if n < NCH:
                        norm_out(img, n, "k", n)
                    if 0 <= n - 1 < NCH:
                        exp_k(img, n - 1)
                act.wait_ge(s_m, img * 7 + 3)
                nc.scalar.activation(ctxg[:], psW[:, 0:P], ACT.Identity, bias=norm[:, 1:2],
                                     scale=norm[:, 0:1]).then_inc(s_m, 1)
                for n in range(C_SLOTS):
                    if 0 <= n - 4 < NCH:
                        act.wait_ge(o_ready, img * NCH + n - 4 + 1)
                        act.wait_ge(s_vsum, img * NCH + n - 4)
                        nc.scalar.activation(sqo[:], psW[:].rearrange("p (t a c) -> p t a c", t=TPC, a=2)[:, :, 0, :],
                                             ACT.Square).then_inc(s_sqo, 1)
                        act.wait_ge(s_x1, img * NCH + max(n - 4 - 1, 0))
                        nc.scalar.copy(y[(n - 4) % 2][:], psW[:].rearrange("p (t a c) -> p t a c", t=TPC, a=2)[:, :, 1, :]
                                       ).then_inc(s_yraw, 1)
                    if 0 <= n - 3 < NCH:
                        act.wait_ge(psx_ready, img * SEQ + seqQ[n - 3] + 1)
                        act.wait_ge(o_ready, img * NCH + n - 3)
                        nc.scalar.copy(qT[:], psX[:]).then_inc(psx_drained, 1)
                    if n < NCH:
                        norm_out(img, n, "q", NCH + n)
                    if 0 <= n - 1 < NCH:
                        act.wait_ge(q_subbed, img * NCH + n - 1 + 1)
                        nc.scalar.activation(q[(n - 1) % 3][:], q[(n - 1) % 3][:], ACT.Exp).then_inc(s_qexp, 1)
                    if 0 <= n - 5 < NCH:
                        act.wait_ge(s_x1, img * NCH + n - 5 + 1)
                        if n - 5 == 0:
                            act.wait_ge(s_red, img)
                            dst = accs
                        else:
                            act.wait_ge(s_accs, img * (NCH - 1) + max(n - 5 - 2, 0))
                            dst = sqx[(n - 5) % 2]
                        nc.scalar.activation(dst[:], X[n - 5][:], ACT.Square).then_inc(s_sqx, 1)

        @block.vector
        def _(dve):
            t = Tally(dve, s_chain)
            t.then(nc.vector.memset(ones[:], 1.0))
            t.then(nc.vector.memset(acc[:], 0.0))
            t.then(nc.vector.memset(nmax[:, 0:1], 3.0e38))
            t.then(nc.vector.memset(ksum[:, 0:1], 0.0))
            dve.wait_ge(s_const, 16 * NCONST)
            t.then(nc.vector.tensor_reduce(mean_w[:, 0:1], wo[:, 0, :], AX.X, ALU.add))
            t.then(nc.vector.tensor_reduce(mean_w[:, 1:2], brow[:, 0, :], AX.X, ALU.add))
            t.then(nc.vector.tensor_scalar(mean_w[:], mean_w[:], 1.0 / C, None, ALU.mult))
            for src, i, f in ((wo, 0, 1.0), (brow, 1, 1.0 / HEADS)):
                ins = nc.vector.tensor_scalar(src[:, 0, :], src[:, 0, :], mean_w[:, i:i + 1], f,
                                              ALU.subtract, ALU.mult)
                ins.then_inc(s_centred, 1)
            dve.wait_ge(s_centred, 2)
            t.then(nc.vector.tensor_scalar(grow[:], grow[:], float(np.sqrt(C)), None, ALU.mult))
            t.then(nc.vector.tensor_tensor(wo[:, 1, :], wo[:, 0, :], grow[:], ALU.mult))
            t.then(nc.vector.tensor_tensor(brow[:, 1, :], brow[:, 0, :], grow[:], ALU.mult))

            def max_k(img, n):
                dve.wait_ge(psk_ready, img * 2 * NCH + n + 1)
                nc.vector.tensor_reduce(nmax_c[:, n:n + 1], psK[:], AX.X, ALU.max, negate=True).then_inc(s_nmc, 1)
                dve.wait_ge(s_nmc, img * NCH + n + 1)
                dve.wait_ge(s_nmax, img * NCH + n)
                nc.vector.tensor_tensor(nmax[:, n + 1:n + 2], nmax[:, n:n + 1], nmax_c[:, n:n + 1],
                                        ALU.min).then_inc(s_nmax, 1)

            def copy_ek(img, n):
                dve.wait_ge(et_ready, img * NCH + n + 1)
                dve.wait_ge(ctx_done, img * NCH + max(n - 1, 0))
                nc.vector.tensor_copy(ek[n % 2][:].rearrange("p t c -> p (t c)"), psW[:, 0:CT]).then_inc(ek_ready, 1)

            def add_up(img, n):
                dve.wait_ge(ctx_done, img * NCH + n + 1)
                dve.wait_ge(s_corr, img * NCH + n + 1)
                dve.wait_ge(acc_done, img * NCH + n)
                nc.vector.scalar_tensor_tensor(ksum[:, n + 1:n + 2], ksum[:, n:n + 1], corr[:, n:n + 1],
                                               ksum_c[:, n:n + 1], ALU.mult, ALU.add)
                nc.vector.scalar_tensor_tensor(
                    acc[:], acc[:], corr[:, n:n + 1], psW[:, CT + 512 * (n % 2):CT + 512 * (n % 2) + C],
                    ALU.mult, ALU.add).then_inc(acc_done, 1)

            with dve.Fori(0, IMGS) as img:
                nc.vector.tensor_copy(norm[:, 0:1], scale1[:, bass.ds(img, 1)])
                nc.vector.tensor_copy(norm[:, 1:2], shift1[:, bass.ds(img, 1)]).then_inc(s_norm, 1)
                for n in range(B_SLOTS):
                    if 0 <= n - 1 < NCH:
                        max_k(img, n - 1)
                    if 0 <= n - 2 < NCH:
                        add_up(img, n - 2)
                    if 0 <= n - 1 < NCH:
                        copy_ek(img, n - 1)
                dve.wait_ge(acc_done, img * NCH + NCH)
                nc.vector.reciprocal(rk[:], ksum[:, NCH:NCH + 1]).then_inc(s_m, 1)
                dve.wait_ge(s_m, img * 7 + 1)
                nc.vector.tensor_scalar(accn[:], acc[:], rk[:], None, ALU.mult).then_inc(s_m, 1)
                dve.wait_ge(s_m, img * 7 + 5)
                nc.vector.tensor_tensor(ctxT[:], psW[:, 512:512 + P], head[:], ALU.mult).then_inc(s_m, 1)
                dve.wait_ge(s_m, img * 7 + 7)
                nc.vector.tensor_tensor(M[:].rearrange("p a c -> p (a c)"), psW[:, 1024:1024 + 2 * C],
                                        brow[:].rearrange("p a c -> p (a c)"), ALU.add).then_inc(s_mready, 1)
                for n in range(C_SLOTS):
                    if 0 <= n - 4 < NCH:
                        m = n - 4
                        dve.wait_ge(s_sqo, img * NCH + m + 1)
                        nc.vector.tensor_reduce(vsum[:, m % 2, :], sqo[:], AX.X, ALU.add).then_inc(s_vsum, 1)
                    if 0 <= n - 1 < NCH:
                        m = n - 1
                        dve.wait_ge(psk_ready, img * 2 * NCH + NCH + m + 1)
                        v = psK[:].rearrange("p (h d) -> p h d", d=DH)
                        nc.vector.tensor_reduce(qmax[:, m % 3, :], v, AX.X, ALU.max).then_inc(s_qmax, 1)
                        dve.wait_ge(s_qmax, img * NCH + m + 1)
                        dve.wait_ge(psx_ready, img * SEQ + (seqQ[m - 3] + 1 if m >= 3 else 0))
                        qv = q[m % 3][:].rearrange("p t (h d) -> p (t h) d", d=DH)
                        mx = qmax[:, m % 3, :].unsqueeze(2).to_broadcast([P, TPC * HEADS, DH])
                        nc.vector.tensor_tensor(qv, v, mx, ALU.subtract).then_inc(q_subbed, 1)
                    if 0 <= n - 4 < NCH:
                        m = n - 4
                        dve.wait_ge(s_rstd, img * NCH + m + 1)
                        dve.wait_ge(s_yraw, img * NCH + m + 1)
                        rs = rstd[:, m % 2, :].unsqueeze(2).to_broadcast([P, TPC, C])
                        nc.vector.tensor_tensor(y[m % 2][:], y[m % 2][:], rs, ALU.mult).then_inc(s_y, 1)
                    if 1 <= n - 6 < NCH:
                        m = n - 6
                        dve.wait_ge(s_sqx, img * NCH + m + 1)
                        dve.wait_ge(s_accs, img * (NCH - 1) + m - 1)
                        nc.vector.tensor_tensor(accs[:], accs[:], sqx[m % 2][:], ALU.add).then_inc(s_accs, 1)
                    if 1 <= n - 5 < NCH:
                        m = n - 5
                        dve.wait_ge(s_x1, img * NCH + m + 1)
                        if m == 1:
                            dve.wait_ge(s_red, img)
                            nc.vector.tensor_tensor(accx[:, ACUT:], X[0][:, ACUT:], X[1][:, ACUT:], ALU.add
                                                    ).then_inc(s_accx_dve, 2)
                        else:
                            dve.wait_ge(s_accx_dve, img * NCH + m)
                            nc.vector.tensor_tensor(accx[:, ACUT:], accx[:, ACUT:], X[m][:, ACUT:], ALU.add
                                                    ).then_inc(s_accx_dve, 1)
                    if 0 <= n - 1 < NCH:
                        m = n - 1
                        dve.wait_ge(s_qexp, img * NCH + m + 1)
                        qv = q[m % 3][:].rearrange("p t (h d) -> p (t h) d", d=DH)
                        nc.vector.tensor_reduce(qsum[:, m % 3, :], qv, AX.X, ALU.add).then_inc(s_qsum, 1)
                        dve.wait_ge(s_qsum, img * NCH + m + 1)
                        nc.vector.reciprocal(qinv[:, m % 3, :], qsum[:, m % 3, :]).then_inc(s_qinv, 1)
                dve.wait_ge(s_accs, (img + 1) * (NCH - 1))
                dve.wait_ge(s_accx, (img + 1) * NCH)
                dve.wait_ge(s_accx_dve, (img + 1) * NCH)
                nc.vector.tensor_reduce(red[:, 0, :], accx[:].rearrange("p t c -> p c t"), AX.X, ALU.add)
                nc.vector.tensor_reduce(red[:, 1, :], accs[:].rearrange("p t c -> p c t"), AX.X, ALU.add
                                        ).then_inc(s_red, 1)
                dve.wait_ge(st_ready, img + 1)
                nc.vector.tensor_copy(sums2[:, :, bass.ds(img, 1)].squeeze(2), psX[:, 0:CT:512]).then_inc(st_taken, 1)

        @block.gpsimd
        def _(pool):
            nc.gpsimd.memset(half[:], -0.5).then_inc(s_half, 1)
            nc.gpsimd.memset(ceps[:], C * LN_EPS).then_inc(s_half, 1)
            pool.wait_ge(s_half, 2)
            with pool.Fori(0, IMGS) as img:
                for n in range(C_SLOTS):
                    if 0 <= n - 4 < NCH:
                        m = n - 4
                        pool.wait_ge(s_vsum, img * NCH + m + 1)
                        nc.gpsimd.tensor_tensor(rstd[:, m % 2, :], vsum[:, m % 2, :], ceps[:],
                                                ALU.add).then_inc(s_rstd1, 1)
                        pool.wait_ge(s_rstd1, img * NCH + m + 1)
                        nc.gpsimd.tensor_tensor(rstd[:, m % 2, :], rstd[:, m % 2, :], half[:],
                                                ALU.pow).then_inc(s_rstd, 1)
                    if 0 <= n - 2 < NCH:
                        m = n - 2
                        pool.wait_ge(s_qinv, img * NCH + m + 1)
                        qv = q[m % 3][:].rearrange("p t (h d) -> p (t h) d", d=DH)
                        iv = qinv[:, m % 3, :].unsqueeze(2).to_broadcast([P, TPC * HEADS, DH])
                        nc.gpsimd.tensor_tensor(qv, qv, iv, ALU.mult).then_inc(s_qn, 1)
                    if 0 <= n - 4 < NCH:
                        m = n - 4
                        pool.wait_ge(s_y, img * NCH + m + 1)
                        nc.gpsimd.tensor_tensor(X[m][:], X[m][:], y[m % 2][:], ALU.add).then_inc(s_x1, 1)
                        pool.wait_ge(s_x1, img * NCH + m + 1)
                        if m == 1:
                            pool.wait_ge(s_red, img)
                            nc.gpsimd.tensor_tensor(accx[:, 0:ACUT], X[0][:, 0:ACUT], X[1][:, 0:ACUT], ALU.add
                                                    ).then_inc(s_accx, 2)
                        elif m > 1:
                            pool.wait_ge(s_accx, img * NCH + m)
                            nc.gpsimd.tensor_tensor(accx[:, 0:ACUT], accx[:, 0:ACUT], X[m][:, 0:ACUT], ALU.add
                                                    ).then_inc(s_accx, 1)


def corner_block(nc, kA, kGA, x1_d, norm_d, ident, group, bln_col, sums2, scale2, shift2, corner):
    HW_ = KS - 1
    WIN = 2 * HW_ + 1
    LO, HI = HW_ * WIN, (HW_ + 1) * WIN
    PIECES = [(0, 15, 5, 3), (3, 16, 0, 3), (6, 0, 3, 5), (11, 1, 0, 2)]
    with ExitStack() as ctx:
        sb = lambda n, s, d=F32: ctx.enter_context(nc.sbuf_tensor(n, s, d))
        ps = lambda n, s, d=F32: ctx.enter_context(nc.psum_tensor(n, s, d))
        sem = lambda n: ctx.enter_context(nc.semaphore(n))
        tok = sb("tok", [P, 2, 2, C])
        win = sb("win", [C, WIN, WIN, IMGS])
        gate = sb("gate", [C, KS, KS, IMGS])
        a = sb("a", [C, KS, KS, IMGS])
        cpow = sb("cpow", [C, KS, KS, IMGS])
        cp1 = sb("cp1", [C, KS, KS, IMGS])
        ka = sb("ka", [C, TAPS])
        kga = sb("kga", [C, TAPS])
        stat = sb("stat2", [P, 2, IMGS])
        var = sb("var2", [P, IMGS])
        cross = sb("cross", [P, IMGS])
        bb = sb("bb", [P, 2])
        half = sb("minus_half2", [P, IMGS])
        rows = sb("norm_rows_sb", [IMGS, 2, C])
        psG = ps("psG2", [P, 512])
        psR = ps("psR", [P, 2, 128])
        psT = [ps(f"psTok{k}", [P, 2, P]) for k in range(2)]
        s_const = sem("c_const")
        s_chain = sem("c_chain")
        s_sums = sem("c_sums")
        s_stat = sem("c_stat")
        s_pow = sem("c_pow")
        s_norm = sem("c_norm_ready")
        s_rows = sem("c_rows")
        s_rout = sem("c_rows_out")
        s_tok = [sem(f"c_tok{k}") for k in range(2)]
        s_turned = sem("c_turned")
        s_win = [sem(f"c_win{k}") for k in range(2)]
        s_gate = sem("c_gate")
        s_sig = sem("c_sigmoids")
        block = ctx.enter_context(nc.Block())

        @block.sync
        def _(sp):
            sp.dma_start(ka[:], kA).then_inc(s_const, 16)
            sp.dma_start(kga[:], kGA).then_inc(s_const, 16)
            for pair in range(IMGS // 2):
                for k in range(2):
                    sp.wait_ge(s_win[k], pair * 8)
                    im = x1_d[pair * 2 + k]
                    for a, r, nr in ((0, HT - HW_, HW_), (1, 0, KS)):
                        at = 0
                        for _, q, j, nj in PIECES:
                            sp.dma_start(tok[at:at + nr * nj, k, a, :], im[q, r:r + nr, j:j + nj, :]
                                         ).then_inc(s_tok[k], 16)
                            at += nr * nj
            sp.wait_ge(s_rows, 2)
            sp.dma_start(norm_d, rows[:]).then_inc(s_rout, 16)
            sp.wait_ge(s_rout, 16)

        @block.gpsimd
        def _(pool):
            nc.gpsimd.memset(half[:], -0.5).then_inc(s_pow, 1)
            pool.wait_ge(s_pow, 1)
            pool.wait_ge(s_stat, 2)
            nc.gpsimd.tensor_tensor(scale2[:], var[:], half[:], ALU.pow).then_inc(s_pow, 1)

        @block.tensor
        def _(pe):
            pe.wait_ge(s_sums, 1)
            nc.tensor.matmul(psG[:, 0:2 * IMGS], group[:], stat[:].rearrange("p a b -> p (a b)"),
                             start=True, stop=True).then_inc(s_sums, 1)
            pe.wait_ge(s_norm, 1)
            nc.tensor.transpose(psR[0:IMGS, 0, :], scale2[:], ident[:])
            nc.tensor.transpose(psR[0:IMGS, 1, :], shift2[:], ident[:]).then_inc(s_rows, 1)
            for pair in range(IMGS // 2):
                for k in range(2):
                    pe.wait_ge(s_tok[k], pair * 128 + 128)
                    pe.wait_ge(s_win[k], pair * 8)
                    nc.tensor.transpose(psT[k][:, 0, 0:LO], tok[0:LO, k, 0, :], ident[0:LO, 0:LO])
                    nc.tensor.transpose(psT[k][:, 1, 0:HI], tok[0:HI, k, 1, :], ident[0:HI, 0:HI]
                                        ).then_inc(s_turned, 1)

        @block.scalar
        def _(act):
            act.wait_ge(s_norm, 1)
            for pair in range(IMGS // 2):
                for k in range(2):
                    img = pair * 2 + k
                    act.wait_ge(s_turned, pair * 2 + k + 1)
                    for half_, rows_, nr in ((0, slice(0, HW_), HW_), (1, slice(HW_, WIN), KS)):
                        at = 0
                        for col, _, _, ncol in PIECES:
                            cols = slice(col, col + ncol)
                            src = psT[k][:, half_, at:at + nr * ncol].rearrange("p (r c) -> p r c", c=ncol)
                            nc.scalar.activation(win[:, rows_, cols, img], src, ACT.Identity,
                                                 bias=shift2[:, img:img + 1], scale=scale2[:, img:img + 1]
                                                 ).then_inc(s_win[k], 1)
                            at += nr * ncol
            flat = lambda z: z[:].rearrange("p a b i -> p (a b i)")
            act.wait_ge(s_gate, TAPS)
            nc.scalar.activation(flat(gate), flat(gate), ACT.Sigmoid).then_inc(s_sig, 1)
            act.wait_ge(s_gate, TAPS + 1)
            nc.scalar.activation(flat(cpow), flat(a), ACT.Sigmoid, scale=-1.0).then_inc(s_sig, 1)
            nc.scalar.activation(flat(corner), flat(a), ACT.Sigmoid).then_inc(s_sig, 1)

        @block.vector
        def _(dve):
            t = Tally(dve, s_chain)
            bln = lambda: bln_col[:]
            t.then(nc.vector.tensor_scalar(cross[:], sums2[:, 0, :], bln(), 2.0, ALU.mult, ALU.mult))
            t.then(nc.vector.tensor_tensor(cross[:], sums2[:, 1, :], cross[:], ALU.add))
            t.then(nc.vector.tensor_scalar(bb[:, 0:1], bln(), float(N), None, ALU.mult))
            t.then(nc.vector.tensor_tensor(bb[:, 1:2], bb[:, 0:1], bln(), ALU.mult))
            t.then(nc.vector.tensor_scalar(stat[:, 0, :], sums2[:, 0, :], bb[:, 0:1], None, ALU.add))
            nc.vector.tensor_scalar(stat[:, 1, :], cross[:], bb[:, 1:2], None, ALU.add).then_inc(s_sums, 1)
            dve.wait_ge(s_sums, 2)
            norm_scale(nc, dve, t, psG, stat, var, s_stat)
            dve.wait_ge(s_pow, 2)
            t.then(nc.vector.tensor_scalar(stat[:, 0, :], stat[:, 0, :], bln(), -1.0, ALU.subtract, ALU.mult))
            nc.vector.tensor_tensor(shift2[:], stat[:, 0, :], scale2[:], ALU.mult).then_inc(s_norm, 1)
            dve.wait_ge(s_rows, 1)
            nc.vector.tensor_copy(rows[:], psR[0:IMGS, :, :]).then_inc(s_rows, 1)
            dve.wait_ge(s_const, 32)
            for k in range(2):
                dve.wait_ge(s_win[k], 8 * (IMGS // 2))
            for u in range(KS):
                for v in range(KS):
                    i = u * KS + v
                    src = win[:, HW_ - u:HW_ - u + KS, HW_ - v:HW_ - v + KS, :].rearrange("p a b i -> p a (b i)")
                    dst = gate[:].rearrange("p a b i -> p a (b i)")
                    if i == 0:
                        ins = nc.vector.tensor_scalar(dst, src, kga[:, 0:1], None, ALU.mult)
                    else:
                        dve.wait_ge(s_gate, i)
                        ins = nc.vector.scalar_tensor_tensor(dst, src, kga[:, i:i + 1], dst, ALU.mult, ALU.add)
                    ins.then_inc(s_gate, 1)
            f3 = lambda z: z[:].rearrange("p a b i -> p (a b) i")
            dve.wait_ge(s_sig, 1)
            nc.vector.tensor_tensor(f3(a), f3(gate), ka[:].unsqueeze(2).to_broadcast([C, TAPS, IMGS]),
                                    ALU.mult).then_inc(s_gate, 1)
            dve.wait_ge(s_sig, 3)
            flat = lambda z: z[:].rearrange("p a b i -> p (a b i)")
            for i in range(3):
                t.then(nc.vector.tensor_scalar(flat(cp1), flat(cpow), 1.0, 1.0 if i else 1.0 / A_FREE,
                                               ALU.add, ALU.mult))
                t.then(nc.vector.tensor_tensor(flat(corner), flat(corner), flat(cp1), ALU.mult))
                t.then(nc.vector.tensor_tensor(flat(cpow), flat(cpow), flat(cpow), ALU.mult))


def layer1(nc, w_out1, b_out1, b_ln, x1_d, wide_d, narrow_d, norm_d, ident, corner, out):
    HQ = [(0, 8), (8, 8)]
    NST = 2 * (NP_ + 1)
    RES = 4
    RING = 4
    with ExitStack() as ctx:
        sb = lambda n, s, d=F32: ctx.enter_context(nc.sbuf_tensor(n, s, d))
        ps = lambda n, s, d=F32: ctx.enter_context(nc.psum_tensor(n, s, d))
        sem = lambda n: ctx.enter_context(nc.semaphore(n))
        xhl = sb("xhl", [P, 2, NP_ + 1, NQ, C], BF16)
        right = sb("right", [P, RING, 2, (NP_ + 1) * NQ, CB], BF16)
        h = sb("h", [P, BR * BC_, C])
        wide = sb("wide", [P, TRING, TC, WIDE], BF16)
        narrow = sb("narrow", [P, TRING, TC, NARROW], BF16)
        stage = [sb(f"stage{k}", [P, HQ[k][1], C]) for k in range(2)]
        tbuf = sb("tbuf", [P, 2, GCH, P])
        ubuf = sb("ubuf", [P, GCH, P])
        nrow = sb("nrow", [P, 2, C])
        w = sb("w1", [C, C])
        bias = sb("bias", [1, C])
        bl = sb("bl", [1, C])
        bias3 = sb("bias3", [1, 3, C], BF16)
        bias_k = sb("bias_k", [3, 1, C], BF16)
        ones3 = sb("ones3", [3, P], BF16)
        psH = ps("psH", [C, BC_, P])
        psO = ps("psO", [P, BC_ * C])
        psC = [ps("psC0", [P, CB, 2, P]), ps("psC1", [P, CB, 2, P]),
               psH[:].rearrange("p (a v) o -> p a v o", v=2),
               psO[:].rearrange("p (a v o) -> p a v o", v=2, o=P)]

        s_const = sem("d_const")
        s_chain = sem("d_chain")
        s_bias = sem("d_bias")
        s_bias_k = sem("d_bias_k")
        s_t = [sem(f"d_table{k}") for k in range(TRING)]
        s_st = [sem(f"d_stage{k}") for k in range(2)]
        s_nrow = sem("d_nrow")
        s_right = sem("d_right")
        s_right_lo = sem("d_right_lo")
        s_res = [sem(f"d_res{k}") for k in range(RES)]
        s_out = [sem(f"d_out{k}") for k in range(RES)]
        s_scaled = sem("d_scaled")
        s_normed = sem("d_normed")
        xh_done = sem("d_xh")
        xl_done = sem("d_xl")
        conv_ready = sem("d_conv")
        conv_half = sem("d_conv_half")
        th_done = sem("d_tanh")
        s_prod = [sem(f"d_prod{k}") for k in range(RING)]
        s_nabs = sem("d_nabs")
        s_exp = sem("d_exp")
        s_ln = sem("d_ln")
        h_done = sem("d_h")
        ht_ready = sem("d_ht_ready")
        ht_evac = sem("d_ht_evac")
        s_fixed = sem("d_fixed")
        o_ready = sem("d_o_ready")
        s_added = sem("d_added")
        block = ctx.enter_context(nc.Block())

        res = tbuf[:].rearrange("p a g c -> p (a g c)").rearrange("p (k e) -> p k e", k=RES)
        hT = ubuf[:].rearrange("p g c -> p (g c)").rearrange("p (k e) -> p k e", k=2)
        FIX = {HT - 3 + y - (NP_ - 1) * BR if y < 3 else y - 3: (NP_ - 1 if y < 3 else 0, y) for y in range(KS)}

        def stage_parts(img, pr, q0, nq):
            def rows(h0, n):
                return x1_d[img, q0:q0 + nq, h0:h0 + n].rearrange("q h j c -> (h j) q c")
            if pr == 0:
                return [(slice(0, PADL * BC_), rows(HT - PADL, PADL)),
                        (slice(PADL * BC_, P), rows(0, BR - PADL))]
            if pr < NP_:
                return [(slice(0, P), rows(pr * BR - PADL, BR))]
            return [(slice(0, PADL * BC_), rows(HT - PADL, PADL)),
                    (slice(PADL * BC_, NARROW_K), rows(0, PADL))]

        NPART = [len(stage_parts(0, pr, 0, 9)) for pr in range(NP_ + 1)]
        CUM = [sum(NPART[:pr + 1]) for pr in range(NP_ + 1)]

        @block.sync
        def _(sp):
            for dst, src in ((w[:], w_out1), (bias[:], b_out1.partition_broadcast(1)),
                             (bl[:], b_ln.rearrange("c o -> o c"))):
                sp.dma_start(dst, src).then_inc(s_const, 16)

            def load_table(part, k):
                sp.dma_start(wide[:, k], wide_d[part].rearrange("p (c e) -> p c e", c=TC)).then_inc(s_t[k], 16)
                sp.dma_start(narrow[0:NARROW_K, k], narrow_d[part].rearrange("p (c e) -> p c e", c=TC)
                             ).then_inc(s_t[k], 16)

            def load_rows(nth, img):
                sp.wait_ge(xl_done, nth * NST)
                sp.dma_start(nrow[:], norm_d[img].partition_broadcast(P)).then_inc(s_nrow, 16)

            def load_stage(nth, img, st):
                pr, hf = st // 2, st % 2
                sp.wait_ge(xl_done, nth * NST + max(st - 1, 0))
                for part, src in stage_parts(img, pr, *HQ[hf]):
                    sp.dma_start(stage[hf][part], src).then_inc(s_st[hf], 16)

            sp.wait_ge(s_chain, 8)
            for i in range(3):
                sp.dma_start(bias_k[i:i + 1, 0, :], bias3[:, i, :]).then_inc(s_bias_k, 16)
            for k in range(TRING):
                load_table(k, k)
            load_rows(0, 0)
            for st in range(NST):
                load_stage(0, 0, st)
            with sp.Fori(0, IMGS) as img:
                nxt = (img + 1) % IMGS
                with sp.Fori(0, NBLK // 2 - 1) as it:
                    for k in range(TRING):
                        sp.wait_ge((conv_half, conv_ready)[k % 2], img * NBLK + it * 2 + k // 2 + 1)
                        load_table(it * TRING + TRING + k, k)
                load_rows(img + 1, nxt)
                load_stage(img + 1, nxt, 0)
                load_stage(img + 1, nxt, 1)
                sp.wait_ge(h_done, img * NGRP + NGRP)

                def load_res(r):
                    k = r % RES
                    if r >= RES:
                        sp.wait_ge(s_out[k], 16 * (img * (BR // RES) + r // RES))
                    src = x1_d[img, :, r:HT:BR].rearrange("q p j c -> p q (j c)")
                    cut = (BC_ - PADL) * C
                    sp.dma_start(res[:, k, 0:cut], src[:, 0:NQ, PADL * C:]).then_inc(s_res[k], 16)
                    sp.dma_start(res[:, k, cut:], src[:, 1:NQ + 1, 0:PADL * C]).then_inc(s_res[k], 16)

                load_res(0)
                load_res(1)
                for r in range(BR + 1):
                    if r >= 1:
                        m = r - 1
                        sp.wait_ge(s_added, img * BR + m + 1)
                        dst = out[img, m:HT:BR].rearrange("p (q s) c -> p q (s c)", s=BC_)
                        sp.dma_start(dst, res[:, m % RES, :]).then_inc(s_out[m % RES], 16)
                    if r + 2 < BR:
                        load_res(r + 2)
                    if r < BR:
                        load_stage(img + 1, nxt, r + 2)
                    if r == BR - 4:
                        sp.wait_ge(conv_ready, img * NBLK + NBLK)
                        for k in range(TRING):
                            load_table(k, k)
            for k in range(RES):
                sp.wait_ge(s_out[k], 16 * IMGS * BR // RES)
            for k in range(TRING):
                sp.wait_ge(s_t[k], 32 * (IMGS * (NBLK // 2) + 1))

        def scale_stage(pool, nth, st):
            pr, hf = st // 2, st % 2
            np_ = P if pr < NP_ else NARROW_K
            if st == 0:
                pool.wait_ge(s_nrow, 16 * nth + 16)
            pool.wait_ge(s_st[hf], nth * (16 * CUM[-1]) + 16 * CUM[pr])
            v = stage[hf][0:np_]
            nc.gpsimd.tensor_tensor(v, v, nrow[0:np_, 0:1, :].to_broadcast([np_, HQ[hf][1], C]),
                                    ALU.mult).then_inc(s_scaled, 1)

        def shift_stage(dve, nth, st):
            pr, hf = st // 2, st % 2
            np_ = P if pr < NP_ else NARROW_K
            dve.wait_ge(s_scaled, nth * NST + st + 1)
            v = stage[hf][0:np_]
            nc.vector.tensor_tensor(v, v, nrow[0:np_, 1:2, :].to_broadcast([np_, HQ[hf][1], C]),
                                    ALU.add).then_inc(s_normed, 1)

        def high_stage(act, nth, st):
            pr, hf = st // 2, st % 2
            np_ = P if pr < NP_ else NARROW_K
            q0, nq = HQ[hf]
            act.wait_ge(s_normed, nth * NST + st + 1)
            nc.scalar.copy(xhl[0:np_, 0, pr, q0:q0 + nq, :], stage[hf][0:np_]).then_inc(xh_done, 1)

        def low_stage(dve, nth, st):
            pr, hf = st // 2, st % 2
            np_ = P if pr < NP_ else NARROW_K
            q0, nq = HQ[hf]
            dve.wait_ge(xh_done, nth * NST + st + 1)
            nc.vector.tensor_tensor(xhl[0:np_, 1, pr, q0:q0 + nq, :], stage[hf][0:np_], xhl[0:np_, 0, pr, q0:q0 + nq, :],
                                    ALU.subtract).then_inc(xl_done, 1)

        @block.gpsimd
        def _(pool):
            for st in range(NST):
                scale_stage(pool, 0, st)
            with pool.Fori(0, IMGS) as img:
                def right_high(tile, cs):
                    dst = tile.rearrange("p (b q) c -> p b q c", q=NQ)
                    src = xhl[:, 0, :, :, cs]
                    nc.gpsimd.tensor_copy(dst[:, :, 0:NQ - 1, :], src[:, :, 1:NQ, :])
                    nc.gpsimd.tensor_copy(dst[:, :, NQ - 1, :], src[:, :, 0, :]).then_inc(s_right, 1)

                with pool.Fori(0, RING) as k:
                    pool.wait_ge(xh_done, img * NST + NST)
                    right_high(right[:, bass.ds(k, 1), 0].squeeze(1), bass.ds(k * CB, CB))
                with pool.Fori(0, NBLK // RING - 1) as it:
                    for k in range(RING):
                        pool.wait_ge(conv_ready, img * NBLK + it * RING + k + 1)
                        right_high(right[:, k, 0], bass.ds(it * (RING * CB) + (RING + k) * CB, CB))
                for st in range(NST):
                    scale_stage(pool, img + 1, st)

        @block.tensor
        def _(pe):
            pe.wait_ge(s_const, 48)
            pe.wait_ge(s_chain, 8)
            pe.wait_ge(s_bias_k, 48)

            def conv_channel(k, ci, tk, c):
                dst = psC[k][:, ci]
                n = 0
                for q, (dp, dq, r0, c0) in enumerate(QUADS):
                    tab = (wide if q < 2 else narrow)[:, tk, ci % TC, QBASE[q]:QBASE[q] + 4 * QSIZE[q]]
                    tab = tab.rearrange("p (a e) -> p a e", a=2)
                    if c0 == 0:
                        o = dst[:, :, r0 * BC_:]
                    elif r0 == 0:
                        o = dst.rearrange("p v (r s) -> p (v r) s", s=BC_)[:, :, c0:]
                    else:
                        o = dst.rearrange("p v (r s) -> p v r s", s=BC_)[:, :, r0:, c0:]
                    for hl, part in ((0, 0), (0, 1), (1, 0)):
                        if dq:
                            lhs = right[:, k, hl, dp * NQ:(dp + NP_) * NQ, ci]
                        else:
                            lhs = xhl[:, hl, dp:dp + NP_, :, bass.ds(c, 1)].rearrange("p a b c -> p (a b c)")
                        mm = nc.tensor.matmul(o, lhs, tab[:, part, :], start=(n == 0), stop=(n == 11))
                        n += 1
                return mm

            with pe.Fori(0, IMGS) as img:
                with pe.Fori(0, NBLK // RING) as it:
                    pe.wait_ge(xh_done, img * NST + NST)
                    pe.wait_ge(xl_done, img * NST + NST)
                    pe.wait_ge(ht_evac, img * BR)
                    pe.wait_ge(s_added, img * BR)
                    for k in range(RING):
                        pe.wait_ge(s_right, img * NBLK + it * RING + k + 1)
                        pe.wait_ge(s_right_lo, img * NBLK + it * RING + k + 1)
                        pe.wait_ge(s_prod[k], img * (NBLK // RING) + it)
                        for ci in range(CB):
                            tk = (k * CB + ci) // TC % TRING
                            use = RING * CB // (TC * TRING)
                            if ci % TC == 0:
                                pe.wait_ge(s_t[tk], img * (NBLK // 2 * 32) + it * (use * 32)
                                           + 32 * (k * CB // (TC * TRING) + 1))
                            mm = conv_channel(k, ci, tk, it * (RING * CB) + k * CB + ci)
                            if ci == TC - 1:
                                mm.then_inc(conv_half, 1)
                        mm.then_inc(conv_ready, 1)
                pe.wait_ge(h_done, img * NGRP + NGRP)
                for r in range(BR + 1):
                    if r < BR:
                        pe.wait_ge(ht_evac, img * BR + r)
                        for s in range(BC_):
                            mm = nc.tensor.transpose(psH[:, s, :], h[:, r * BC_ + s, :], ident[:])
                        mm.then_inc(ht_ready, 1)
                    if r >= 1:
                        m = r - 1
                        pe.wait_ge(ht_evac, img * BR + m + 1)
                        if m in FIX:
                            nfix = sum(1 for z in FIX if z <= m)
                            pe.wait_ge(s_fixed, img * KS + nfix)
                        pe.wait_ge(s_added, img * BR + m)
                        for b in range(2):
                            nc.tensor.matmul(psO[:, b * 512:(b + 1) * 512].rearrange("p (s c) -> p s c", c=C),
                                             ones3[:], bias_k[:].to_broadcast([3, 4, C]), start=True, stop=False)
                            for s in range(4 * b, 4 * b + 4):
                                mm = nc.tensor.matmul(psO[:, s * C:(s + 1) * C], hT[:, m % 2, s * P:(s + 1) * P],
                                                      w[:], start=False, stop=(s % 4 == 3))
                        mm.then_inc(o_ready, 1)

        @block.scalar
        def _(act):
            for st in range(NST):
                if st == 0:
                    act.wait_ge(s_chain, 2)
                high_stage(act, 0, st)
            with act.Fori(0, IMGS) as img:
                u = ubuf[:].rearrange("p g c -> p (g c)")

                def exp_ln(g):
                    act.wait_ge(s_nabs, img * NGRP + g + 1)
                    nc.scalar.activation(u, u, ACT.Exp).then_inc(s_exp, 1)
                    act.wait_ge(s_exp, img * NGRP + g + 1)
                    nc.scalar.activation(u, u, ACT.Ln, bias=1.0).then_inc(s_ln, 1)

                for g in range(NGRP):
                    for b in range(BPG):
                        if b == 2 and g >= 1:
                            exp_ln(g - 1)
                        blk = g * BPG + b
                        act.wait_ge(conv_ready, img * NBLK + blk + 1)
                        if blk == 0:
                            for k in range(RES):
                                act.wait_ge(s_out[k], 16 * (img * (BR // RES)))
                        if b == 0 and g >= 2:
                            act.wait_ge(h_done, img * NGRP + g - 1)
                        nc.scalar.activation(tbuf[:, g % 2, b * CB:(b + 1) * CB, :], psC[blk % RING][:, :, 1, :],
                                             ACT.Tanh, scale=0.5).then_inc(th_done, 1)
                exp_ln(NGRP - 1)
                act.wait_ge(conv_ready, img * NBLK + NBLK)
                for r in range(NST):
                    if r < BR:
                        act.wait_ge(ht_ready, img * BR + r + 1)
                        act.wait_ge(o_ready, img * BR + max(r - 1, 0))
                        nc.scalar.activation(hT[:, r % 2, :], psH[:].rearrange("p s c -> p (s c)"), ACT.Copy,
                                             bias=A_FREE * H_EPS, scale=A_FREE).then_inc(ht_evac, 1)
                    high_stage(act, img + 1, r)

        @block.vector
        def _(dve):
            t = Tally(dve, s_chain)
            t.then(nc.vector.memset(narrow[:].rearrange("p a c e -> p (a c e)"), 0.0))
            for a in range(2):
                t.then(nc.vector.memset(xhl[:, a, NP_].rearrange("p q c -> p (q c)"), 0.0))
            t.then(nc.vector.memset(ones3[:], 1.0))
            dve.wait_ge(s_const, 48)
            t.then(nc.vector.tensor_tensor(bias[:], bias[:], bl[:], ALU.add))
            for i in range(3):
                ins = nc.vector.tensor_copy(bias3[:, i, :], bias[:])
                if i == 2:
                    t.then(ins)
                else:
                    ins.then_inc(s_bias, 1)
                    dve.wait_ge(s_bias, i + 1)
                    t.then(nc.vector.tensor_tensor(bias[:], bias[:], bias3[:, i, :], ALU.subtract))
            for st in range(NST):
                shift_stage(dve, 0, st)
                low_stage(dve, 0, st)

            def product(img, g, b):
                blk = g * BPG + b
                dve.wait_ge(th_done, img * NBLK + blk + 1)
                tb = tbuf[:, g % 2, b * CB:(b + 1) * CB, :]
                nc.vector.scalar_tensor_tensor(tb, tb, 1.0, psC[blk % RING][:, :, 0, :], ALU.add, ALU.mult
                                               ).then_inc(s_prod[blk % RING], 1)
                if blk + RING < NBLK:
                    right_low(img, blk + RING)

            def negative_abs(img, g):
                for k in range(RING):
                    dve.wait_ge(s_prod[k], img * (NBLK // RING) + (g + 1) * (BPG // RING))
                tb = tbuf[:, g % 2].rearrange("p g c -> p (g c)")
                nc.vector.scalar_tensor_tensor(ubuf[:].rearrange("p g c -> p (g c)"), tb, -1.0, tb,
                                               ALU.mult, ALU.min).then_inc(s_nabs, 1)

            def softplus(img, g):
                dve.wait_ge(s_ln, img * NGRP + g + 1)
                hv = h[:, :, g * GCH:(g + 1) * GCH].rearrange("p o c -> p c o")
                nc.vector.scalar_tensor_tensor(hv, tbuf[:, g % 2], 0.0, ubuf[:], ALU.max, ALU.add
                                               ).then_inc(h_done, 1)

            def right_low(img, blk):
                k = blk % RING
                dst = right[:, k, 1].rearrange("p (b q) c -> p b q c", q=NQ)
                src = xhl[:, 1, :, :, blk * CB:(blk + 1) * CB]
                if blk >= RING:
                    dve.wait_ge(conv_ready, img * NBLK + blk - RING + 1)
                nc.vector.tensor_copy(dst[:, :, 0:NQ - 1, :], src[:, :, 1:NQ, :])
                nc.vector.tensor_copy(dst[:, :, NQ - 1, :], src[:, :, 0, :]).then_inc(s_right_lo, 1)

            with dve.Fori(0, IMGS) as img:
                dve.wait_ge(xl_done, img * NST + NST)
                for k in range(RING):
                    right_low(img, k)
                for g in range(NGRP):
                    product(img, g, 0)
                    product(img, g, 1)
                    if g >= 1:
                        softplus(img, g - 1)
                    product(img, g, 2)
                    product(img, g, 3)
                    negative_abs(img, g)
                softplus(img, NGRP - 1)
                nfix = 0
                for r in range(NST):
                    shift_stage(dve, img + 1, r)
                    if r in FIX:
                        pr, yy = FIX[r]
                        dve.wait_ge(ht_evac, img * BR + r + 1)
                        cor = corner[:, yy, :, bass.ds(img, 1)].squeeze(2)
                        last = hT[:, r % 2, 5 * P + pr * NQ + NQ - 1:8 * P:P]
                        first = hT[:, r % 2, pr * NQ:4 * P:P]
                        nc.vector.tensor_tensor(last, last, cor[:, 0:3], ALU.mult)
                        nc.vector.tensor_tensor(first, first, cor[:, 3:7], ALU.mult).then_inc(s_fixed, 1)
                    if r < BR:
                        k = r % RES
                        dve.wait_ge(o_ready, img * BR + r + 1)
                        dve.wait_ge(s_res[k], 32 * (img * (BR // RES) + r // RES + 1))
                        nc.vector.tensor_tensor(res[:, k, :], psO[:], res[:, k, :], ALU.add).then_inc(s_added, 1)
                    low_stage(dve, img + 1, r)


def kernel(x, L0_conv_w_qkv, L0_conv_w_out, L0_conv_b_out, L0_conv_g_ln, L0_conv_b_ln, L1_conv_A_kernel,
           L1_conv_B_kernel, L1_conv_gate_A_kernel, L1_conv_gate_B_kernel, L1_conv_W_out, L1_conv_b_out):
    import concourse.bacc as bacc
    from concourse.bass_utils import run_bass_kernel_spmd

    f = lambda a: np.ascontiguousarray(np.asarray(a))
    taps_first = lambda k: np.ascontiguousarray(np.asarray(k).reshape(C, TAPS).T)
    arrays = {
        "x": f(x).reshape(IMGS, N, C),
        "w_qkv": f(L0_conv_w_qkv), "w_out0": f(L0_conv_w_out), "b_out0": f(L0_conv_b_out),
        "g_ln": f(L0_conv_g_ln).reshape(C), "b_ln": f(L0_conv_b_ln).reshape(C, 1),
        "kB": taps_first(L1_conv_B_kernel), "kGB": taps_first(L1_conv_gate_B_kernel),
        "kA": f(L1_conv_A_kernel).reshape(C, TAPS), "kGA": f(L1_conv_gate_A_kernel).reshape(C, TAPS),
        "w_out1": f(L1_conv_W_out), "b_out1": f(L1_conv_b_out),
        "ident": np.eye(P, dtype=np.float32),
        "group": np.kron(np.eye(C // GROUP), np.full((GROUP, GROUP), 1.0 / (GROUP * N))).astype(np.float32),
        "head": np.kron(np.eye(HEADS), np.full((DH, DH), DH ** -0.5)).astype(np.float32),
        "sel": selection_table(),
    }
    nc = bacc.Bacc("TRN2", target_bir_lowering=False, num_devices=1)
    args = [nc.dram_tensor("in_" + k, a.shape, mybir.dt.from_np(a.dtype), kind="ExternalInput").ap()
            for k, a in arrays.items()]
    out = nc.dram_tensor("out", (IMGS, HT, WD, C), F32, kind="ExternalOutput").ap()
    build(nc, *args, out)
    r = run_bass_kernel_spmd(nc, [{"in_" + k: a for k, a in arrays.items()}], core_ids=[0])
    return r.results[0]["out"]
```
